# Optimizing a Trainium2 kernel written in Bass

```python
import numpy as np
import jax
import jax.numpy as jnp

def _softmax(x, axis=-1):
    return jax.nn.softmax(x, axis=axis)

def _gelu(x):
    return jax.nn.gelu(x, approximate=True)

def _silu(x):
    return jax.nn.silu(x)

def _sigmoid(x):
    return jax.nn.sigmoid(x)

def _layernorm(x, axis=-1, eps=1e-05):
    m = jnp.mean(x, axis=axis, keepdims=True)
    v = jnp.var(x, axis=axis, keepdims=True)
    return (x - m) / jnp.sqrt(v + eps)

def _scatter_add(tgt, idx, src, axis=0):
    return tgt.at[idx].add(src)

def _segment_sum(src, seg, n):
    return jax.ops.segment_sum(src, seg, n)
kernel_name = 'mk_recurrent_d1_jaxref_r8_524661'

def setup_inputs(seed: int=0):
    np.random.seed(seed)
    _w = jnp.asarray

    def _L0_attn_setup():
        import jax, jax.numpy as jnp
        import numpy as np

        def _rotate_every_two(x):
            x1 = x[..., ::2]
            x2 = x[..., 1::2]
            return jnp.stack((-x2, x1), axis=-1).reshape(x.shape)
        key = jax.random.key(seed)
        ks = jax.random.split(key, 6)
        B, S, D = (2, 256, 128)
        w = lambda k, shape: jax.random.normal(k, shape, dtype=jnp.float32) * 0.02
        return {'x': jax.random.normal(ks[0], (B, S, D), dtype=jnp.float32), 'Wq': w(ks[1], (D, D)), 'bq': jnp.zeros((D,), jnp.float32), 'Wk': w(ks[2], (D, D)), 'bk': jnp.zeros((D,), jnp.float32), 'Wv': w(ks[3], (D, 2 * D)), 'bv': jnp.zeros((2 * D,), jnp.float32), 'Wg': w(ks[4], (D, 2 * D)), 'bg': jnp.zeros((2 * D,), jnp.float32), 'Wo': w(ks[5], (2 * D, D)), 'bo': jnp.zeros((D,), jnp.float32)}
    _L0_attn_in = _L0_attn_setup()

    def _L0_ffn_setup():
        import jax, jax.numpy as jnp
        import numpy as np
        D_MODEL = 128
        N_HEADS = 16
        D_HEAD = D_MODEL // N_HEADS
        N_EXPERTS = 8
        TOP_K = 2
        D_FF = 256
        EPS = 1e-06

        def rmsnorm(x, w):
            return x * jax.lax.rsqrt(jnp.mean(x * x, axis=-1, keepdims=True) + EPS) * w

        def swiglu(x, w_gate, w_up, w_down):
            return jax.nn.silu(x @ w_gate) * (x @ w_up) @ w_down
        key = jax.random.key(seed)
        ks = jax.random.split(key, 16)
        s = 0.02
        B, S = (2, 256)
        return {'X': jax.random.normal(ks[0], (B, S, D_MODEL), dtype=jnp.float32), 'norm1_w': jnp.ones((D_MODEL,), jnp.float32), 'norm2_w': jnp.ones((D_MODEL,), jnp.float32), 'wq': jax.random.normal(ks[1], (D_MODEL, D_MODEL), jnp.float32) * s, 'wk': jax.random.normal(ks[2], (D_MODEL, D_MODEL), jnp.float32) * s, 'wv': jax.random.normal(ks[3], (D_MODEL, D_MODEL), jnp.float32) * s, 'wo': jax.random.normal(ks[4], (D_MODEL, D_MODEL), jnp.float32) * s, 'router_w': jax.random.normal(ks[5], (D_MODEL, N_EXPERTS), jnp.float32) * s, 'sh_gate': jax.random.normal(ks[6], (D_MODEL, D_FF), jnp.float32) * s, 'sh_up': jax.random.normal(ks[7], (D_MODEL, D_FF), jnp.float32) * s, 'sh_down': jax.random.normal(ks[8], (D_FF, D_MODEL), jnp.float32) * s, 'e_gate': jax.random.normal(ks[9], (N_EXPERTS, D_MODEL, D_FF), jnp.float32) * s, 'e_up': jax.random.normal(ks[10], (N_EXPERTS, D_MODEL, D_FF), jnp.float32) * s, 'e_down': jax.random.normal(ks[11], (N_EXPERTS, D_FF, D_MODEL), jnp.float32) * s}
    _L0_ffn_in = _L0_ffn_setup()
    _d = {'L0_attn_x': _L0_attn_in['x'], 'L0_attn_Wq': _L0_attn_in['Wq'], 'L0_attn_bq': _L0_attn_in['bq'], 'L0_attn_Wk': _L0_attn_in['Wk'], 'L0_attn_bk': _L0_attn_in['bk'], 'L0_attn_Wv': _L0_attn_in['Wv'], 'L0_attn_bv': _L0_attn_in['bv'], 'L0_attn_Wg': _L0_attn_in['Wg'], 'L0_attn_bg': _L0_attn_in['bg'], 'L0_attn_Wo': _L0_attn_in['Wo'], 'L0_attn_bo': _L0_attn_in['bo'], 'L0_ffn_norm1_w': _L0_ffn_in['norm1_w'], 'L0_ffn_norm2_w': _L0_ffn_in['norm2_w'], 'L0_ffn_wq': _L0_ffn_in['wq'], 'L0_ffn_wk': _L0_ffn_in['wk'], 'L0_ffn_wv': _L0_ffn_in['wv'], 'L0_ffn_wo': _L0_ffn_in['wo'], 'L0_ffn_router_w': _L0_ffn_in['router_w'], 'L0_ffn_sh_gate': _L0_ffn_in['sh_gate'], 'L0_ffn_sh_up': _L0_ffn_in['sh_up'], 'L0_ffn_sh_down': _L0_ffn_in['sh_down'], 'L0_ffn_e_gate': _L0_ffn_in['e_gate'], 'L0_ffn_e_up': _L0_ffn_in['e_up'], 'L0_ffn_e_down': _L0_ffn_in['e_down']}
    _x0 = _d['L0_attn_x']
    _d['L0_attn_x'] = jax.random.normal(jax.random.fold_in(jax.random.key(seed), 1), (16, 512, 128), dtype=_x0.dtype)
    del _x0
    return _d

def reference(L0_attn_x, L0_attn_Wq, L0_attn_bq, L0_attn_Wk, L0_attn_bk, L0_attn_Wv, L0_attn_bv, L0_attn_Wg, L0_attn_bg, L0_attn_Wo, L0_attn_bo, L0_ffn_norm1_w, L0_ffn_norm2_w, L0_ffn_wq, L0_ffn_wk, L0_ffn_wv, L0_ffn_wo, L0_ffn_router_w, L0_ffn_sh_gate, L0_ffn_sh_up, L0_ffn_sh_down, L0_ffn_e_gate, L0_ffn_e_up, L0_ffn_e_down):

    def _L0_attn_ref(x, Wq, bq, Wk, bk, Wv, bv, Wg, bg, Wo, bo):
        import jax, jax.numpy as jnp
        import numpy as np

        def _rotate_every_two(x):
            x1 = x[..., ::2]
            x2 = x[..., 1::2]
            return jnp.stack((-x2, x1), axis=-1).reshape(x.shape)
        B, S, D = x.shape
        H = 16
        key_dim = D // H
        head_dim = 2 * D // H
        scaling = key_dim ** (-0.5)
        angle = 1.0 / 10000.0 ** jnp.linspace(0.0, 1.0, key_dim // 2)
        angle = jnp.repeat(angle, 2).astype(jnp.float32)
        decay = jnp.log(1.0 - 2.0 ** (-5.0 - jnp.arange(H, dtype=jnp.float32)))
        idx = jnp.arange(S, dtype=jnp.float32)
        sin = jnp.sin(idx[:, None] * angle[None, :])
        cos = jnp.cos(idx[:, None] * angle[None, :])
        diff = idx[:, None] - idx[None, :]
        mask = jnp.where(diff >= 0, jnp.exp(decay[:, None, None] * diff), 0.0)
        mask = mask / jnp.sqrt(mask.sum(-1, keepdims=True))
        q = (x @ Wq + bq).reshape(B, S, H, key_dim).transpose(0, 2, 1, 3)
        k = ((x @ Wk + bk) * scaling).reshape(B, S, H, key_dim).transpose(0, 2, 1, 3)
        v = x @ Wv + bv
        g = x @ Wg + bg
        qr = q * cos + _rotate_every_two(q) * sin
        kr = k * cos + _rotate_every_two(k) * sin
        vr = v.reshape(B, S, H, head_dim).transpose(0, 2, 1, 3)
        qk = jnp.einsum('bhsd,bhtd->bhst', qr, kr) * mask
        denom = jnp.clip(jnp.abs(jax.lax.stop_gradient(qk).sum(-1, keepdims=True)), 1.0, None)
        qk = qk / denom
        out = jnp.einsum('bhst,bhtd->bhsd', qk, vr).transpose(0, 2, 1, 3)
        mu = out.mean(-1, keepdims=True)
        var = ((out - mu) ** 2).mean(-1, keepdims=True)
        out = (out - mu) / jnp.sqrt(var + 1e-05)
        out = out.reshape(B, S, H * head_dim)
        out = jax.nn.silu(g) * out
        return out @ Wo + bo

    def _L0_ffn_ref(X, norm1_w, norm2_w, wq, wk, wv, wo, router_w, sh_gate, sh_up, sh_down, e_gate, e_up, e_down):
        import jax, jax.numpy as jnp
        import numpy as np
        D_MODEL = 128
        N_HEADS = 16
        D_HEAD = D_MODEL // N_HEADS
        N_EXPERTS = 8
        TOP_K = 2
        D_FF = 256
        EPS = 1e-06

        def rmsnorm(x, w):
            return x * jax.lax.rsqrt(jnp.mean(x * x, axis=-1, keepdims=True) + EPS) * w

        def swiglu(x, w_gate, w_up, w_down):
            return jax.nn.silu(x @ w_gate) * (x @ w_up) @ w_down
        B, S, d = X.shape
        scale = 1.0 / jnp.sqrt(jnp.asarray(D_HEAD, X.dtype))
        h = rmsnorm(X, norm1_w)
        q = (h @ wq).reshape(B, S, N_HEADS, D_HEAD)
        k = (h @ wk).reshape(B, S, N_HEADS, D_HEAD)
        v = (h @ wv).reshape(B, S, N_HEADS, D_HEAD)
        scores = jnp.einsum('bshd,bthd->bhst', q, k) * scale
        attn = jax.nn.softmax(scores, axis=-1)
        ctx = jnp.einsum('bhst,bthd->bshd', attn, v).reshape(B, S, d)
        X = X + ctx @ wo
        h2 = rmsnorm(X, norm2_w).reshape(B * S, d)
        logits = h2 @ router_w
        probs = jax.nn.softmax(logits, axis=-1)
        topw, topi = jax.lax.top_k(probs, TOP_K)
        topw = jax.nn.softmax(topw, axis=-1)
        combine = jnp.sum(jax.nn.one_hot(topi, N_EXPERTS, dtype=h2.dtype) * topw[..., None], axis=1)
        shared = swiglu(h2, sh_gate, sh_up, sh_down)
        gate = jnp.einsum('td,edf->etf', h2, e_gate)
        up = jnp.einsum('td,edf->etf', h2, e_up)
        eout = jnp.einsum('etf,efd->etd', jax.nn.silu(gate) * up, e_down)
        spec = jnp.einsum('etd,te->td', eout, combine)
        moe_out = (shared + spec).reshape(B, S, d)
        return X + moe_out
    x = L0_attn_x
    xn = _layernorm(x, axis=-1)
    s = _L0_attn_ref(xn, L0_attn_Wq, L0_attn_bq, L0_attn_Wk, L0_attn_bk, L0_attn_Wv, L0_attn_bv, L0_attn_Wg, L0_attn_bg, L0_attn_Wo, L0_attn_bo)
    g = _silu(_L0_ffn_ref(xn, L0_ffn_norm1_w, L0_ffn_norm2_w, L0_ffn_wq, L0_ffn_wk, L0_ffn_wv, L0_ffn_wo, L0_ffn_router_w, L0_ffn_sh_gate, L0_ffn_sh_up, L0_ffn_sh_down, L0_ffn_e_gate, L0_ffn_e_up, L0_ffn_e_down))
    x = x + s * g
    return x

_drawn_inputs = setup_inputs


def setup_inputs(seed=0):
    import zlib

    import numpy as np

    out = dict(_drawn_inputs(seed))
    spreads = {'L0_attn_bq': (0.0, 0.773),
     'L0_attn_bk': (0.0, 0.469),
     'L0_attn_bv': (0.0, 0.486),
     'L0_attn_bg': (0.0, 0.8),
     'L0_attn_bo': (0.0, 0.1),
     'L0_ffn_norm1_w': (1.0, 0.6),
     'L0_ffn_norm2_w': (1.0, 0.6)}
    factors = {'L0_attn_Wk': 3.131,
     'L0_attn_Wv': 3.065,
     'L0_ffn_wq': 8.0,
     'L0_ffn_wk': 8.0,
     'L0_ffn_wv': 8.0,
     'L0_ffn_wo': 8.0,
     'L0_ffn_router_w': 8.0,
     'L0_ffn_sh_gate': 8.0,
     'L0_ffn_sh_up': 8.0,
     'L0_ffn_sh_down': 8.0,
     'L0_ffn_e_gate': 8.0,
     'L0_ffn_e_up': 8.0,
     'L0_ffn_e_down': 8.0}
    for name, (base, spread) in spreads.items():
        noise = np.random.default_rng([zlib.crc32(name.encode()), seed]).standard_normal(out[name].shape)
        drawn = base * np.exp(spread * noise) if base else spread * noise
        out[name] = jnp.asarray(drawn.astype(out[name].dtype))
    for name, factor in factors.items():
        out[name] = (out[name] * factor).astype(out[name].dtype)
    return out
```

```python
from contextlib import ExitStack

import numpy as np

import concourse.bass as bass
from concourse import mybir

ALU = mybir.AluOpType
ACT = mybir.ActivationFunctionType
F32 = mybir.dt.float32
U32 = mybir.dt.uint32
AX_X = mybir.AxisListType.X

P = 128
B, S, D = 16, 512, 128
NT = S // P
H = 16
DK = D // H
DV = 2 * D // H
G = 4
HG = H // G
SLOT = 32
E = 8
FF = 256
NF = FF // P
UNITS = (E + 1) * NF
DV1 = DV + 1
DK1 = DK + 1
LN_EPS, RMS_EPS, GN_EPS = 1e-5, 1e-6, 1e-5


def shape_tables():
    f = np.float32
    angle = np.repeat((1.0 / 10000.0 ** np.linspace(0.0, 1.0, DK // 2)).astype(f), 2)
    arg = (np.arange(S, dtype=f)[:, None] * angle[None, :]).astype(f).astype(np.float64)
    sign = np.where(np.arange(DK) % 2 == 0, -1.0, 1.0)
    cos = np.tile(np.cos(arg).T, (H, 1)).astype(f)
    sin = np.tile((np.sin(arg) * sign).T, (H, 1)).astype(f)
    decay = np.log1p(-(2.0 ** (-5.0 - np.arange(H))))
    i = np.arange(P)
    diff = i[None, :] - i[:, None]
    mask = np.where(diff[:, None, :] >= 0, np.exp(decay[None, :, None] * np.maximum(diff, 0)[:, None, :]), 0.0)
    qdec = np.repeat(np.exp(decay[:, None] * (i[None, :] + 1)), DK, axis=0)
    kdec = np.repeat(np.exp(decay[None, :] * (P - 1 - i[:, None])), DK, axis=1)
    cdec = np.repeat(np.exp(decay * P), DK)[:, None]
    bd = (np.arange(D)[:, None] // DK == np.arange(H * DV1)[None, :] // DV1)
    a = np.arange(S)
    sums = -np.expm1(decay[None, :] * (a[:, None] + 1)) / -np.expm1(decay)[None, :]
    nrm = np.sqrt(sums).reshape(NT, P, H).transpose(1, 0, 2).reshape(P, NT * H)
    return {
        "cos": cos, "sin": sin, "mask": mask.reshape(P, H * P), "qdec": qdec, "kdec": kdec, "cdec": cdec,
        "bd": bd, "nrm": nrm, "ident": np.eye(P), "iota": np.tile(np.arange(E), (P, NT)),
    }


class Signal:

    def __init__(self, sem, per):
        self.sem, self.per = sem, per

    def at(self, b, k):
        return b * self.per + k

    def count(self, b, k):
        return self.sem, self.at(b, k)

    def before(self, b):
        return self.sem, self.at(b, 0)


def bank_uses():
    front = ["xnT", "hT", "rq", "rqs", "rk", "rks", "aq", "ak", "av"] + [f"vg{c}" for c in range(NT)]
    front += ["kT"] + [f"st{c}" for c in range(NT - 1)]
    uses = [(n, i % 5) for i, n in enumerate(front)]
    for g in range(G):
        for m in range(HG):
            uses.append((f"rs{g}{m}", (g * HG + m) % 3))
            if m == 0:
                uses.append((f"U{g}", 3 + g % 2))
    uses += [("yT0", 0), ("yT1", 1), ("sp", 2)]
    uses += [(f"mx{h}_{i}", (h * NT + i) % 4) for h in range(H) for i in range(NT)]
    uses += [("mT", 4)]
    n = 0
    for g in range(G):
        uses.append((f"O{g}", 3))
        for j in range(NT):
            for m in range(HG):
                uses.append((f"sc{g}{j}{m}", n % 3))
                n += 1
        uses.append((f"OT{g}", 4))
    uses += [("ctxT", 0), ("xp", 1), ("h2T", 2), ("lg", 3), ("wT", 4)]
    for u in range(UNITS):
        uses += [(f"ga{u}", 5), (f"up{u}", 6)]
    uses += [("moe", 7), ("mo", 5)]
    bank, index, count = {}, {}, [0] * 8
    for name, k in uses:
        bank[name], index[name] = k, count[k]
        count[k] += 1
    return bank, index, count


def build(nc, ins, tabs, out):
    with ExitStack() as ctx:
        def sb(name, shape, dt=F32):
            return ctx.enter_context(nc.sbuf_tensor(name, shape, dt))

        def sig(name, per):
            return Signal(ctx.enter_context(nc.semaphore(name)), per)

        BANK, INDEX, COUNT = bank_uses()
        psum = ctx.enter_context(nc.psum_tensor("psum", [P, 8, 512], F32))
        filled = [sig(f"bank{k}_filled", COUNT[k]) for k in range(8)]
        drained = [sig(f"bank{k}_drained", COUNT[k]) for k in range(8)]

        def bankof(use):
            return psum[:, BANK[use], :]

        ident = sb("ident", [P, P])
        cos, sin = sb("cos", [P, S]), sb("sin", [P, S])
        mask = sb("mask", [P, H, P])
        qdec, kdec, cdec = sb("qdec", [P, P]), sb("kdec", [P, D]), sb("cdec", [P, 1])
        bd = sb("bd", [P, H * DV1])
        nrm = sb("nrm", [P, NT * H])
        iota = sb("iota", [P, NT, E])
        w_rq, w_rqs, w_rk, w_rks = (sb(n, [P, D]) for n in ("w_rq", "w_rqs", "w_rk", "w_rks"))
        w_vg = sb("w_vg", [P, 4 * D])
        w_ro = sb("w_ro", [P, 2, D])
        w_aq, w_ak, w_av, w_ao = (sb(n, [P, D]) for n in ("w_aq", "w_ak", "w_av", "w_ao"))
        w_rt = sb("w_rt", [P, E])
        w_gate = sb("w_gate", [P, E + 1, FF])
        w_up = sb("w_up", [P, E + 1, FF])
        w_down = sb("w_down", [P, UNITS, D])
        colb = sb("colb", [P, 6])
        b_vg = sb("b_vg", [P, 4 * D])
        b_o = sb("b_o", [P, D])
        neghalf = sb("neghalf", [P, 64])
        consts = sb("consts", [P, 4, NT])
        x_in, x_res = sb("x_in", [P, NT, D]), sb("x_res", [P, NT, D])
        stats = sb("stats", [P, NT, 6])
        mv = sb("mv", [P, NT, 2])
        lnc = sb("lnc", [P, 6, NT])
        xn, hn = sb("xn", [P, NT, D]), sb("hn", [P, NT, D])
        xnT, hT = sb("xnT", [P, S]), sb("hT", [P, S])
        rot = sb("rot", [P, 4, S])
        qr, kr = sb("qr", [P, S]), sb("kr", [P, S])
        aq, ak = sb("aq", [P, S]), sb("ak", [P, S])
        rqp, rkp = sb("rqp", [P, G, S]), sb("rkp", [P, G, S])
        aqp, akp = sb("aqp", [P, G, S]), sb("akp", [P, G, S])
        qd = sb("qd", [P, NT, P])
        kd = sb("kd", [P, NT, D])
        state = sb("state", [P, NT - 1, H * DV1])
        vr = sb("vr", [P, NT, H, DV1])
        gin = sb("gin", [P, NT, 2 * D])
        th = sb("th", [P, NT, 2 * D])
        U = sb("U", [P, NT, H, DV1])
        sq = sb("sq", [P, NT, 2 * D])
        gn = sb("gn", [P, 6, NT * H])
        yT = rot[:, 0:2, :]
        s_out = sb("s_out", [P, NT, D])
        vt = sb("vt", [P, NT, H, DK1])
        mx = sb("mx", [P, NT, H])
        mTs = sb("mTs", [H, S])
        PT = sb("PT", [P, 8, S])
        rsc = PT[:, 0:3, :]
        Os = sb("Os", [P, S])
        rec = sb("rec", [P, NT, HG])
        ctxt = sb("ctxt", [P, NT, D])
        ctxT = hT
        X1 = sb("X1", [P, NT, D])
        rs2 = sb("rs2", [P, 4, NT])
        h2 = hn
        h2T = sb("h2T", [P, S])
        lg = sb("lg", [P, 4, NT, E])
        rt = sb("rt", [P, 8, NT])
        top = sb("top", [P, NT, 8])
        topi = sb("topi", [P, NT, 8], U32)
        topf = sb("topf", [P, NT, 8])
        wTs = sb("wTs", [E, S])
        wbc = sb("wbc", [P, E, S])
        hid = sb("hid", [P, 3, S])
        moT = sb("moT", [P, S])
        Y, tY = sb("Y", [P, NT, D]), sb("tY", [P, NT, D])
        d_rq, d_rk, d_aq, d_ak = (nc.dram_tensor(n, [P, S], F32, kind="Internal").ap()
                                  for n in ("d_rq", "d_rk", "d_aq", "d_ak"))
        d_m = nc.dram_tensor("d_m", [H, S], F32, kind="Internal").ap()
        d_w = nc.dram_tensor("d_w", [E, S], F32, kind="Internal").ap()

        loaded = sig("weights_loaded", 0)
        scaled = sig("weights_scaled", 0)
        inited = sig("constants_written", 0)
        x_ld, x_res_ld = sig("x_loaded", 16), sig("x_res_loaded", 16)
        mv_done = sig("mean_var_done", NT)
        lnf = sig("norm_factors_step", 8)
        xn_done, hn_done = sig("xn_done", NT), sig("hn_done", NT)
        xnT_done, hT_done = sig("xnT_done", 1), sig("hT_done", 1)
        rot_done = sig("rotary_terms_done", 4)
        qk_done = sig("rotary_sums_done", 2)
        aqk_done = sig("attention_qk_done", 2)
        spilled = sig("qk_spilled", 64)
        slot_r, slot_a = sig("retention_qk_slotted", 16 * 2 * HG), sig("attention_qk_slotted", 16 * 2 * HG)
        qd_done = sig("decayed_q_done", 1)
        kd_done = sig("decayed_k_done", 1)
        vr_done, gin_done, vt_done = sig("retention_v_done", NT), None, None
        th_done, gs_done = sig("gate_tanh_done", 1), sig("gate_silu_done", 1)
        st_done = sig("state_step_done", NT - 2)
        rsc_done = sig("masked_scores_done", G * NT)
        U_done = sig("retention_sums_done", G)
        gnp = sig("group_norm_pool_step", 3)
        gnv = sig("group_norm_vector_step", 9)
        yT_done, s_done = sig("yT_done", 2), sig("retention_out_done", 1)
        mx_done = sig("row_max_done", H * NT)
        mTs_done = sig("neg_max_transposed", 1)
        m_spilled, m_slotted = sig("neg_max_spilled", 16), sig("neg_max_slotted", 16 * HG)
        exp_done = sig("exp_done", H * NT)
        pv_done = sig("pv_step_done", G * (NT - 1))
        Os_done = sig("attention_sums_done", G)
        rec_done, ctx_done = sig("softmax_recip_done", G), sig("context_done", G)
        ctxT_done = sig("contextT_done", 1)
        X1_done = sig("residual_done", 1)
        sq2_done = sig("residual_squares_done", NT)
        rs2_done = sig("rms2_factor_step", 3)
        h2_done = sig("h2_done", NT)
        h2T_done = sig("h2T_done", 1)
        lgv = sig("router_vector_step", 12)
        lgw = sig("router_weights_step", 2)
        pv_ret = sig("retention_sums_step", G * (HG - 1))
        lga = sig("router_exp_step", 2)
        wT_done = sig("combineT_done", 1)
        w_spilled, w_bcast = sig("combine_spilled", 16), sig("combine_broadcast", 16)
        th2, act2, hid2 = sig("expert_tanh_done", UNITS), sig("expert_silu_done", UNITS), sig("expert_hidden_done", UNITS)
        hidw = sig("expert_hidden_weighted", UNITS - NF)
        down_done = sig("down_step_done", UNITS - 1)
        moT_done = sig("moeT_done", 1)
        Yv, tY_done = sig("final_vector_step", 3), sig("final_tanh_done", 1)
        stored = sig("output_stored", 16)

        def bank_free(use, b):
            k = BANK[use]
            return drained[k].sem, drained[k].at(b, INDEX[use])

        def bank_full(use, b):
            k = BANK[use]
            return filled[k].sem, filled[k].at(b, INDEX[use] + 1)

        def bank_read(use, b):
            k = BANK[use]
            return drained[k].sem, drained[k].at(b, INDEX[use] + 1)

        def full(use):
            return filled[BANK[use]].sem, 1

        def read(use):
            return drained[BANK[use]].sem, 1

        n_loads = [0]
        block = ctx.enter_context(nc.Block())

        @block.sync
        def _(sp):
            def ld(dst, src):
                sp.dma_start(dst, src).then_inc(loaded.sem, 16)
                n_loads[0] += 1

            def row(ap, n):
                return ap.rearrange("(a n) -> a n", a=1).to_broadcast([P, n])

            ld(ident[:], tabs["ident"])
            for dst, name in ((cos, "cos"), (sin, "sin"), (qdec, "qdec"), (kdec, "kdec"), (cdec, "cdec"), (bd, "bd"),
                              (nrm, "nrm")):
                ld(dst[:], tabs[name])
            ld(mask[:], tabs["mask"].rearrange("p (h s) -> p h s", h=H))
            ld(iota[:], tabs["iota"].rearrange("p (i e) -> p i e", e=E))
            for dst, name in ((w_rq, "Wq"), (w_rqs, "Wq_swapped"), (w_rk, "Wk"), (w_rks, "Wk_swapped")):
                ld(dst[:], ins[name])
            ld(w_vg[:, 0:2 * D], ins["Wv"])
            ld(w_vg[:, 2 * D:4 * D], ins["Wg"])
            ld(w_ro[:], ins["Wo"].rearrange("(a p) n -> p a n", p=P))
            for dst, name in ((w_aq, "wq"), (w_ak, "wk"), (w_av, "wv"), (w_ao, "wo"), (w_rt, "router_w")):
                ld(dst[:], ins[name])
            ld(w_gate[:, 0, :], ins["sh_gate"])
            ld(w_up[:, 0, :], ins["sh_up"])
            ld(w_down[:, 0:NF, :], ins["sh_down"].rearrange("(a p) n -> p a n", p=P))
            ld(w_gate[:, 1:, :], ins["e_gate"].rearrange("e p f -> p e f"))
            ld(w_up[:, 1:, :], ins["e_up"].rearrange("e p f -> p e f"))
            ld(w_down[:, NF:, :], ins["e_down"].rearrange("e (a p) n -> p (e a) n", p=P))
            ld(colb[:], ins["columns"])
            ld(b_vg[:, 0:2 * D], bass.AP(ins["bv"].tensor, 0, [[0, P], [1, 2 * D]]))
            ld(b_vg[:, 2 * D:4 * D], bass.AP(ins["bg"].tensor, 0, [[0, P], [1, 2 * D]]))
            ld(b_o[:], bass.AP(ins["bo"].tensor, 0, [[0, P], [1, D]]))

            def batch(b):
                x_b = ins["x"][bass.ds(b, 1)].rearrange("o (i p) d -> p (o i) d", p=P)
                o_b = out[bass.ds(b, 1)].rearrange("o (i p) d -> p (o i) d", p=P)
                sp.wait_ge(*hn_done.before(b))
                sp.dma_start(x_in[:], x_b).then_inc(x_ld.sem, 16)

                for k, (s, dst) in enumerate(((qr, d_rq), (kr, d_rk))):
                    sp.wait_ge(*qk_done.count(b, k + 1))
                    sp.dma_start(dst, s[:]).then_inc(spilled.sem, 16)
                for k, (s, dst) in enumerate(((aq, d_aq), (ak, d_ak))):
                    sp.wait_ge(*bank_read(("aq", "ak")[k], b))
                    sp.dma_start(dst, s[:]).then_inc(spilled.sem, 16)
                sp.wait_ge(*spilled.count(b, 64))
                for src, dst in ((d_rq, rqp), (d_rk, rkp)):
                    for m in range(HG):
                        sp.dma_start(dst[SLOT * m:SLOT * m + DK, :, :],
                                     src.rearrange("(g m d) s -> m d g s", g=G, m=HG)[m]).then_inc(slot_r.sem, 16)
                for src, dst in ((d_aq, aqp), (d_ak, akp)):
                    for m in range(HG):
                        sp.dma_start(dst[SLOT * m:SLOT * m + DK, :, :],
                                     src.rearrange("(g m d) s -> m d g s", g=G, m=HG)[m]).then_inc(slot_a.sem, 16)
                sp.wait_ge(*bank_read("mT", b))
                sp.dma_start(d_m, mTs[:]).then_inc(m_spilled.sem, 16)
                sp.wait_ge(*m_spilled.count(b, 16))
                for m in range(HG):
                    sp.dma_start(aqp[SLOT * m + DK:SLOT * m + DK + 1, :, :],
                                 d_m.rearrange("(g m) s -> m g s", m=HG)[m:m + 1]).then_inc(m_slotted.sem, 16)
                sp.wait_ge(*bank_read("wT", b))
                sp.dma_start(d_w, wTs[:]).then_inc(w_spilled.sem, 16)
                sp.wait_ge(*w_spilled.count(b, 16))
                sp.wait_ge(*hidw.before(b))
                sp.dma_start(wbc[:], bass.AP(d_w.tensor, 0, [[0, P], [S, E], [1, S]])).then_inc(w_bcast.sem, 16)
                sp.wait_ge(*Yv.before(b))
                sp.dma_start(x_res[:], x_b).then_inc(x_res_ld.sem, 16)
                sp.wait_ge(*Yv.count(b, 3))
                sp.dma_start(o_b, Y[:]).then_inc(stored.sem, 16)
            batch(0)
            with sp.Fori(1, B) as b:
                batch(b)
            sp.wait_ge(stored.sem, 16 * B)

        @block.tensor
        def _(pe):
            pe.wait_ge(loaded.sem, 16 * n_loads[0])
            pe.wait_ge(scaled.sem, 2)
            pe.wait_ge(inited.sem, 9)
            def batch(b):
                def mm(o, l, r, start=True, stop=True, **kw):
                    return pe.matmul(o, l, r, start=start, stop=stop, **kw)

                def four(use, src):
                    pe.wait_ge(*bank_free(use, b))
                    for i in range(NT):
                        last = pe.transpose(bankof(use)[:, i * P:(i + 1) * P], src(i), ident[:])
                    last.then_inc(*full(use))

                pe.wait_ge(*xn_done.count(b, NT))
                four("xnT", lambda i: xn[:, i, :])
                pe.wait_ge(*hn_done.count(b, NT))
                four("hT", lambda i: hn[:, i, :])
                pe.wait_ge(*bank_read("xnT", b))
                for use, w in (("rq", w_rq), ("rqs", w_rqs), ("rk", w_rk), ("rks", w_rks)):
                    pe.wait_ge(*bank_free(use, b))
                    mm(bankof(use), w[:], xnT[:]).then_inc(*full(use))
                pe.wait_ge(*bank_read("hT", b))
                for use, w in (("aq", w_aq), ("ak", w_ak)):
                    pe.wait_ge(*bank_free(use, b))
                    mm(bankof(use), w[:], hT[:]).then_inc(*full(use))
                pe.wait_ge(*bank_free("av", b))
                for i in range(NT):
                    last = mm(bankof("av")[:, i * D:(i + 1) * D], hT[:, i * P:(i + 1) * P], w_av[:])
                last.then_inc(*full("av"))
                for c in range(NT):
                    pe.wait_ge(*bank_free(f"vg{c}", b))
                    mm(bankof(f"vg{c}"), xnT[:, c * P:(c + 1) * P], w_vg[:]).then_inc(*full(f"vg{c}"))
                pe.wait_ge(*qk_done.count(b, 2))
                four("kT", lambda i: kr[:, i * P:(i + 1) * P])
                pe.wait_ge(*bank_read("kT", b))
                for c in range(NT - 1):
                    pe.wait_ge(*bank_free(f"st{c}", b))
                    pe.wait_ge(*vr_done.count(b, c + 1))
                    mm(bankof(f"st{c}")[:, 0:H * DV1], kd[:, c, :],
                            vr[:, c, :, :].rearrange("p h v -> p (h v)")).then_inc(*full(f"st{c}"))
                pe.wait_ge(*slot_r.count(b, slot_r.per))
                pe.wait_ge(*st_done.count(b, st_done.per))
                pe.wait_ge(*vr_done.count(b, NT))
                pe.wait_ge(*qd_done.count(b, 1))

                def ret_scores(g, m):
                    use = f"rs{g}{m}"
                    pe.wait_ge(*bank_free(use, b))
                    r = slice(SLOT * m, SLOT * m + DK)
                    for c in range(NT):
                        last = mm(bankof(use)[:, c * P:(c + 1) * P], rkp[r, g, c * P:(c + 1) * P],
                                  rqp[r, g, c * P:(c + 1) * P])
                    last.then_inc(*full(use))

                def ret_sums(g, m):
                    use, w = f"U{g}", HG * DV1
                    if m == 0:
                        pe.wait_ge(*bank_free(use, b))
                        for c in range(1, NT):
                            mm(bankof(use)[:, c * w:(c + 1) * w], qd[SLOT * g:SLOT * g + SLOT, c, :],
                               state[SLOT * g:SLOT * g + SLOT, c - 1, g * w:(g + 1) * w],
                               start=(c == 1), stop=False, skip_group_check=True)
                    pe.wait_ge(*bank_read(f"rs{g}{m}", b))
                    for c in range(NT):
                        last = mm(bankof(use)[:, c * w + m * DV1:c * w + (m + 1) * DV1],
                                  rsc[:, (g * HG + m) % 3, c * P:(c + 1) * P], vr[:, c, g * HG + m, :],
                                  start=False, stop=(m == HG - 1), skip_group_check=True)
                    if m == HG - 1:
                        last.then_inc(*full(use))
                    else:
                        last.then_inc(pv_ret.sem, 1)

                steps = [(g, m) for g in range(G) for m in range(HG)]
                ret_scores(*steps[0])
                for n, (g, m) in enumerate(steps):
                    if n + 1 < len(steps):
                        ret_scores(*steps[n + 1])
                    ret_sums(g, m)
                pe.wait_ge(*gnv.count(b, gnv.per))
                for a in range(2):
                    four(f"yT{a}", lambda i: sq[:, i, a * D:(a + 1) * D])
                pe.wait_ge(*bank_free("sp", b))
                pe.wait_ge(*bank_read("yT0", b))
                pe.wait_ge(*bank_read("yT1", b))
                for i in range(NT):
                    for a in range(2):
                        last = mm(bankof("sp")[:, i * D:(i + 1) * D], yT[:, a, i * P:(i + 1) * P], w_ro[:, a, :],
                                  start=(a == 0), stop=(a == 1))
                last.then_inc(*full("sp"))

                pe.wait_ge(*slot_a.count(b, slot_a.per))
                for h in range(H):
                    g, m = divmod(h, HG)
                    r = slice(SLOT * m, SLOT * m + DK)
                    for i in range(NT):
                        use = f"mx{h}_{i}"
                        pe.wait_ge(*bank_free(use, b))
                        mm(bankof(use), aqp[r, g, i * P:(i + 1) * P], akp[r, g, :]).then_inc(*full(use))
                for i in range(NT):
                    pe.wait_ge(*bank_read(f"mx{H - 1}_{i}", b))
                pe.wait_ge(*bank_free("mT", b))
                for i in range(NT):
                    last = pe.transpose(bankof("mT")[0:H, i * P:(i + 1) * P], mx[:, i, :], ident[:])
                last.then_inc(*full("mT"))
                pe.wait_ge(*m_slotted.count(b, m_slotted.per))
                pe.wait_ge(*bank_read("av", b))

                def att_scores(g, j):
                    for m in range(HG):
                        use = f"sc{g}{j}{m}"
                        r = slice(SLOT * m, SLOT * m + DK + 1)
                        pe.wait_ge(*bank_free(use, b))
                        mm(bankof(use), akp[r, g, j * P:(j + 1) * P], aqp[r, g, :]).then_inc(*full(use))

                def att_pv(g, j):
                    if j == 0:
                        pe.wait_ge(*bank_free(f"O{g}", b))
                    for m in range(1, HG):
                        pe.wait_ge(*bank_read(f"sc{g}{j}{m}", b))
                    for m in range(HG):
                        last = mm(bankof(f"O{g}")[SLOT * m:SLOT * m + DK1, :], vt[:, j, g * HG + m, :],
                                  PT[:, (j % 2) * HG + m, :], start=(j == 0), stop=(j == NT - 1))
                    if j == NT - 1:
                        last.then_inc(*full(f"O{g}"))
                    else:
                        last.then_inc(pv_done.sem, 1)

                def att_out(g):
                    pe.wait_ge(*bank_read(f"O{g}", b))
                    four(f"OT{g}", lambda i: Os[:, i * P:(i + 1) * P])

                steps = [(g, j) for g in range(G) for j in range(NT)]
                att_scores(*steps[0])
                for n, (g, j) in enumerate(steps):
                    if n + 1 < len(steps):
                        att_scores(*steps[n + 1])
                    att_pv(g, j)
                    if j == 0 and g > 0:
                        att_out(g - 1)
                att_out(G - 1)
                pe.wait_ge(*bank_read(f"OT{G - 1}", b))
                four("ctxT", lambda i: ctxt[:, i, :])
                pe.wait_ge(*bank_read("ctxT", b))
                pe.wait_ge(*bank_free("xp", b))
                for i in range(NT):
                    last = mm(bankof("xp")[:, i * D:(i + 1) * D], ctxT[:, i * P:(i + 1) * P], w_ao[:])
                last.then_inc(*full("xp"))
                pe.wait_ge(*h2_done.count(b, NT))
                four("h2T", lambda i: h2[:, i, :])
                pe.wait_ge(*bank_read("h2T", b))
                pe.wait_ge(*bank_free("lg", b))
                for i in range(NT):
                    last = mm(bankof("lg")[:, i * E:(i + 1) * E], h2T[:, i * P:(i + 1) * P], w_rt[:])
                last.then_inc(*full("lg"))

                def gate_up(u):
                    e, f = divmod(u, NF)
                    for use, w in ((f"ga{u}", w_gate), (f"up{u}", w_up)):
                        pe.wait_ge(*bank_free(use, b))
                        mm(bankof(use), w[:, e, f * P:(f + 1) * P], h2T[:]).then_inc(*full(use))

                def down(u):
                    if u == 0:
                        pe.wait_ge(*bank_free("moe", b))
                    if u < NF:
                        pe.wait_ge(*bank_read(f"up{u}", b))
                    else:
                        pe.wait_ge(*hidw.count(b, u - NF + 1))
                    last = mm(bankof("moe"), w_down[:, u, :], hid[:, u % 3, :], start=(u == 0), stop=(u == UNITS - 1))
                    if u == UNITS - 1:
                        last.then_inc(*full("moe"))
                    else:
                        last.then_inc(down_done.sem, 1)

                gate_up(0)
                gate_up(1)
                pe.wait_ge(*lgv.count(b, lgv.per))
                pe.wait_ge(*bank_free("wT", b))
                for i in range(NT):
                    last = pe.transpose(bankof("wT")[0:E, i * P:(i + 1) * P], lg[:, 3, i, :], ident[:])
                last.then_inc(*full("wT"))
                for u in range(2, UNITS):
                    gate_up(u)
                    down(u - 2)
                down(UNITS - 2)
                down(UNITS - 1)
                pe.wait_ge(*bank_read("moe", b))
                four("mo", lambda i: moT[:, i * P:(i + 1) * P])
            batch(0)
            with pe.Fori(1, B) as b:
                batch(b)

        @block.vector
        def _(v):
            v.memset(neghalf[:], -0.5).then_inc(inited.sem, 1)
            for n, value in enumerate((LN_EPS, RMS_EPS, 1.0 / D, float(DK) ** -0.5)):
                v.memset(consts[:, n, :], value).then_inc(inited.sem, 1)
            v.memset(vr[:, :, :, DV:DV1], 1.0).then_inc(inited.sem, 1)
            v.memset(vt[:, :, :, DK:DK1], 1.0).then_inc(inited.sem, 1)
            v.memset(akp[:], 1.0).then_inc(inited.sem, 1)
            v.memset(Y[:], 0.0).then_inc(inited.sem, 1)
            v.wait_ge(loaded.sem, 16 * n_loads[0])
            v.tensor_scalar(w_down[:], w_down[:], 0.5, None, ALU.mult).then_inc(scaled.sem, 1)
            v.tensor_scalar(w_ro[:], w_ro[:], 0.5, None, ALU.mult).then_inc(scaled.sem, 1)
            v.wait_ge(inited.sem, 9)
            def batch(b):
                v.wait_ge(*lnf.before(b))
                v.wait_ge(*x_ld.count(b, 16))
                for i in range(NT):
                    v.bn_stats(stats[:, i, :], x_in[:, i, :])
                v.drain()
                for i in range(NT):
                    v.bn_aggr(mv[:, i, :], stats[:, i, :]).then_inc(mv_done.sem, 1)
                v.wait_ge(*lnf.count(b, 2))
                v.wait_ge(*filled[BANK["xnT"]].before(b))
                v.wait_ge(*drained[BANK["xp"]].before(b))
                for i in range(NT):
                    v.tensor_scalar(xn[:, i, :], x_in[:, i, :], mv[:, i, 0:1], lnc[:, 1, i:i + 1],
                                    ALU.subtract, ALU.mult).then_inc(xn_done.sem, 1)
                v.wait_ge(*lnf.count(b, 7))
                v.wait_ge(*filled[BANK["hT"]].before(b))
                for i in range(NT):
                    v.tensor_scalar(hn[:, i, :], x_in[:, i, :], mv[:, i, 0:1], lnc[:, 5, i:i + 1],
                                    ALU.subtract, ALU.mult).then_inc(hn_done.sem, 1)
                v.wait_ge(*qk_done.before(b))
                for n, (use, tab) in enumerate((("rq", cos), ("rqs", sin), ("rk", cos), ("rks", sin))):
                    v.wait_ge(*bank_full(use, b))
                    v.scalar_tensor_tensor(rot[:, n, :], bankof(use), colb[:, n:n + 1], tab[:], ALU.add,
                                                 ALU.mult).then_inc(*read(use))
                v.wait_ge(*drained[BANK["U0"]].before(b))
                v.wait_ge(*gs_done.before(b))
                v.wait_ge(*th_done.before(b))
                for c in range(NT):
                    v.wait_ge(*bank_full(f"vg{c}", b))
                    v.tensor_tensor(vr[:, c, :, 0:DV], bankof(f"vg{c}")[:, 0:2 * D].rearrange("p (h v) -> p h v", h=H),
                                    b_vg[:, 0:2 * D].rearrange("p (h v) -> p h v", h=H), ALU.add).then_inc(vr_done.sem, 1)
                    v.tensor_tensor(gin[:, c, :], bankof(f"vg{c}")[:, 2 * D:4 * D], b_vg[:, 2 * D:4 * D], ALU.add).then_inc(*read(f"vg{c}"))
                v.wait_ge(*bank_full("kT", b))
                v.tensor_tensor(kd[:], bankof("kT").rearrange("p (i d) -> p i d", i=NT),
                                      kdec[:].unsqueeze(1).to_broadcast([P, NT, D]), ALU.mult).then_inc(*read("kT"))
                for c in range(NT - 1):
                    v.wait_ge(*bank_full(f"st{c}", b))
                    v.tensor_tensor(state[:, c, :], bankof(f"st{c}")[:, 0:H * DV1], bd[:], ALU.mult).then_inc(*read(f"st{c}"))
                    if c > 0:
                        v.wait_ge(*bank_read(f"st{c}", b))
                        if c > 1:
                            v.wait_ge(*st_done.count(b, c - 1))
                        v.scalar_tensor_tensor(state[:, c, :], state[:, c - 1, :], cdec[:, 0:1], state[:, c, :],
                                               ALU.mult, ALU.add).then_inc(st_done.sem, 1)
                for g in range(G):
                    for m in range(HG):
                        n = g * HG + m
                        use = f"rs{g}{m}"
                        v.wait_ge(*bank_full(use, b))
                        if n >= 3:
                            g3, m3 = divmod(n - 3, HG)
                            if m3 == HG - 1:
                                v.wait_ge(*bank_full(f"U{g3}", b))
                            else:
                                v.wait_ge(*pv_ret.count(b, g3 * (HG - 1) + m3 + 1))
                        v.tensor_tensor(rsc[:, n % 3, :].rearrange("p (c s) -> p c s", c=NT),
                                              bankof(use).rearrange("p (c s) -> p c s", c=NT),
                                              mask[:, n, :].unsqueeze(1).to_broadcast([P, NT, P]), ALU.mult).then_inc(*read(use))
                v.wait_ge(*th_done.count(b, 1))
                flat = "p i n -> p (i n)"
                v.scalar_tensor_tensor(gin[:].rearrange(flat), th[:].rearrange(flat), 1.0, gin[:].rearrange(flat),
                                       ALU.add, ALU.mult).then_inc(gs_done.sem, 1)
                for g in range(G):
                    v.wait_ge(*bank_read(f"U{g}", b))
                r = U[:, :, :, DV].rearrange("p c h -> p c h")
                c3 = lambda n: gn[:, n, :].rearrange("p (c h) -> p c h", h=H)
                v.tensor_reduce(c3(0), U[:, :, :, 0:DV], AX_X, ALU.add).then_inc(gnv.sem, 1)
                v.scalar_tensor_tensor(c3(1), r, -1.0, r, ALU.mult, ALU.max).then_inc(gnv.sem, 1)
                v.wait_ge(*gnv.count(b, 1))
                v.tensor_scalar(gn[:, 0, :], gn[:, 0, :], 1.0 / DV, None, ALU.mult).then_inc(gnv.sem, 1)
                v.wait_ge(*gnv.count(b, 2))
                v.tensor_tensor(gn[:, 1, :], gn[:, 1, :], nrm[:], ALU.max).then_inc(gnv.sem, 1)
                v.wait_ge(*gnv.count(b, 4))
                v.scalar_tensor_tensor(gn[:, 2, :], gn[:, 1, :], GN_EPS, gn[:, 1, :], ALU.mult,
                                       ALU.mult).then_inc(gnv.sem, 1)
                v.wait_ge(*gnp.count(b, 2))
                v.tensor_reduce(gn[:, 3, :], sq[:].rearrange("p c (h v) -> p (c h) v", v=DV), AX_X,
                                ALU.add).then_inc(gnv.sem, 1)
                v.wait_ge(*gnv.count(b, 6))
                v.scalar_tensor_tensor(gn[:, 4, :], gn[:, 3, :], 1.0 / DV, gn[:, 2, :], ALU.mult,
                                       ALU.add).then_inc(gnv.sem, 1)
                v.wait_ge(*gnp.count(b, 3))
                v.wait_ge(*gnv.count(b, 7))
                v.wait_ge(*gs_done.count(b, 1))
                hv = "p c (h v) -> p (c h) v"
                v.tensor_tensor(sq[:].rearrange(hv, v=DV), th[:].rearrange(hv, v=DV),
                                gn[:, 5, :].unsqueeze(2).to_broadcast([P, NT * H, DV]), ALU.mult).then_inc(gnv.sem, 1)
                v.wait_ge(*gnv.count(b, 8))
                v.tensor_tensor(sq[:], sq[:], gin[:], ALU.mult).then_inc(gnv.sem, 1)
                v.wait_ge(*bank_full("sp", b))
                v.wait_ge(*Yv.before(b))
                v.tensor_tensor(s_out[:], bankof("sp").rearrange("p (i d) -> p i d", i=NT),
                                      b_o[:].unsqueeze(1).to_broadcast([P, NT, D]), ALU.add).then_inc(*read("sp"))
                v.wait_ge(*filled[BANK["mT"]].before(b))
                for h in range(H):
                    for i in range(NT):
                        use = f"mx{h}_{i}"
                        v.wait_ge(*bank_full(use, b))
                        v.tensor_reduce(mx[:, i, h:h + 1], bankof(use), AX_X, ALU.max).then_inc(*read(use))
                for g in range(G):
                    use = f"OT{g}"
                    v.wait_ge(*bank_full(use, b))
                    o = bankof(use).rearrange("p (i m w) -> p i m w", i=NT, w=SLOT)
                    if g:
                        v.wait_ge(*bank_read(f"OT{g - 1}", b))
                    else:
                        v.wait_ge(*drained[BANK["OT0"]].before(b))
                        v.wait_ge(*drained[BANK["ctxT"]].before(b))
                    v.reciprocal(rec[:], o[:, :, :, DK]).then_inc(rec_done.sem, 1)
                    v.wait_ge(*rec_done.count(b, g + 1))
                    v.tensor_tensor(ctxt[:, :, g * HG * DK:(g + 1) * HG * DK].rearrange("p i (m d) -> p i m d", d=DK),
                                          o[:, :, :, 0:DK], rec[:].unsqueeze(3).to_broadcast([P, NT, HG, DK]), ALU.mult).then_inc(*read(use))
                v.wait_ge(*bank_full("xp", b))
                v.tensor_tensor(X1[:], xn[:], bankof("xp").rearrange("p (i d) -> p i d", i=NT), ALU.add).then_inc(*read("xp"))
                v.wait_ge(*rs2_done.count(b, 3))
                v.wait_ge(*bank_read("xp", b))
                for i in range(NT):
                    v.tensor_scalar(h2[:, i, :], X1[:, i, :], rs2[:, 2, i:i + 1], None, ALU.mult).then_inc(h2_done.sem, 1)
                bc = lambda a: a.unsqueeze(2).to_broadcast([P, NT, E])
                v.wait_ge(*bank_full("lg", b))
                lgp = bankof("lg")[:, 0:NT * E].rearrange("p (i e) -> p i e", e=E)
                v.tensor_reduce(rt[:, 0, :], lgp, AX_X, ALU.max).then_inc(lgv.sem, 1)
                v.wait_ge(*lgv.count(b, 1))
                v.tensor_tensor(lg[:, 0, :, :], lgp, bc(rt[:, 0, :]), ALU.subtract).then_inc(*read("lg"))
                v.wait_ge(*lga.count(b, 1))
                v.tensor_reduce(rt[:, 1, :], lg[:, 1, :, :], AX_X, ALU.add).then_inc(lgv.sem, 1)
                v.wait_ge(*lgv.count(b, 2))
                v.reciprocal(rt[:, 2, :], rt[:, 1, :]).then_inc(lgv.sem, 1)
                v.wait_ge(*lgv.count(b, 3))
                v.tensor_tensor(lg[:, 1, :, :], lg[:, 1, :, :], bc(rt[:, 2, :]), ALU.mult)
                v.drain()
                for i in range(NT):
                    ins_ = v.max(top[:, i, :], lg[:, 1, i, :])
                v.drain()
                for i in range(NT):
                    ins_ = v.max_index(topi[:, i, :], top[:, i, :], lg[:, 1, i, :])
                ins_.then_inc(lgv.sem, 1)
                v.wait_ge(*lgv.count(b, 4))
                v.tensor_copy(topf[:], topi[:]).then_inc(lgv.sem, 1)
                v.wait_ge(*lgv.count(b, 5))
                v.tensor_tensor(rt[:, 3, :], top[:, :, 1], top[:, :, 0], ALU.subtract).then_inc(lgv.sem, 1)
                v.wait_ge(*lgv.count(b, 6))
                v.wait_ge(*lga.count(b, 2))
                v.tensor_scalar(rt[:, 5, :], rt[:, 4, :], 1.0, None, ALU.add).then_inc(lgv.sem, 1)
                v.wait_ge(*lgv.count(b, 7))
                v.reciprocal(rt[:, 6, :], rt[:, 5, :]).then_inc(lgv.sem, 1)
                v.wait_ge(*lgv.count(b, 8))
                v.tensor_tensor(rt[:, 7, :], rt[:, 4, :], rt[:, 6, :], ALU.mult).then_inc(lgv.sem, 1)
                v.wait_ge(*lgv.count(b, 9))
                v.tensor_tensor(lg[:, 2, :, :], iota[:], bc(topf[:, :, 0]), ALU.is_equal).then_inc(lgv.sem, 1)
                v.wait_ge(*lgv.count(b, 10))
                v.tensor_tensor(lg[:, 3, :, :], iota[:], bc(topf[:, :, 1]), ALU.is_equal).then_inc(lgv.sem, 1)
                v.wait_ge(*lgv.count(b, 11))
                v.tensor_tensor(lg[:, 2, :, :], lg[:, 2, :, :], bc(rt[:, 6, :]), ALU.mult).then_inc(lgw.sem, 1)
                v.tensor_tensor(lg[:, 3, :, :], lg[:, 3, :, :], bc(rt[:, 7, :]), ALU.mult).then_inc(lgw.sem, 1)
                v.wait_ge(*lgw.count(b, 2))
                v.tensor_tensor(lg[:, 3, :, :], lg[:, 2, :, :], lg[:, 3, :, :], ALU.add).then_inc(lgv.sem, 1)
                for u in range(UNITS):
                    v.wait_ge(*th2.count(b, u + 1))
                    v.wait_ge(*bank_full(f"up{u}", b))
                    t = hid[:, u % 3, :]
                    v.scalar_tensor_tensor(t, t, 1.0, bankof(f"ga{u}"), ALU.add, ALU.mult).then_inc(*read(f"ga{u}"))
                    v.wait_ge(*bank_read(f"ga{u}", b))
                    v.tensor_tensor(t, t, bankof(f"up{u}"), ALU.mult).then_inc(*read(f"up{u}"))
                v.wait_ge(*bank_full("mo", b))
                v.wait_ge(*stored.before(b))
                v.tensor_tensor(Y[:], X1[:], bankof("mo").rearrange("p (i d) -> p i d", i=NT), ALU.add).then_inc(*read("mo"))
                v.wait_ge(*tY_done.count(b, 1))
                v.scalar_tensor_tensor(Y[:].rearrange(flat), tY[:].rearrange(flat), 1.0, Y[:].rearrange(flat), ALU.add,
                                       ALU.mult).then_inc(Yv.sem, 1)
                v.wait_ge(*Yv.count(b, 1))
                v.scalar_tensor_tensor(Y[:].rearrange(flat), Y[:].rearrange(flat), 0.5, s_out[:].rearrange(flat), ALU.mult,
                                       ALU.mult).then_inc(Yv.sem, 1)
                v.wait_ge(*x_res_ld.count(b, 16))
                v.wait_ge(*Yv.count(b, 2))
                v.tensor_tensor(Y[:], Y[:], x_res[:], ALU.add).then_inc(Yv.sem, 1)
            batch(0)
            with v.Fori(1, B) as b:
                batch(b)

        @block.scalar
        def _(a):
            a.wait_ge(loaded.sem, 16 * n_loads[0])
            def attention_sums(g, b):
                a.wait_ge(*bank_full(f"O{g}", b))
                if g:
                    a.wait_ge(*bank_full(f"OT{g - 1}", b))
                a.copy(Os[:], bankof(f"O{g}")).then_inc(*read(f"O{g}"))

            def batch(b):
                a.wait_ge(*bank_full("xnT", b))
                a.copy(xnT[:], bankof("xnT")).then_inc(*read("xnT"))
                a.wait_ge(*bank_full("hT", b))
                a.activation(hT[:], bankof("hT"), ACT.Identity, scale=colb[:, 4:5]).then_inc(*read("hT"))
                a.wait_ge(*spilled.before(b))
                a.wait_ge(*bank_full("aq", b))
                a.mul(aq[:], bankof("aq"), float(DK) ** -0.5).then_inc(*read("aq"))
                a.wait_ge(*bank_full("ak", b))
                a.copy(ak[:], bankof("ak")).then_inc(*read("ak"))
                a.wait_ge(*pv_done.before(b))
                a.wait_ge(*bank_full("av", b))
                a.copy(vt[:, :, :, 0:DK], bankof("av").rearrange("p (i h d) -> p i h d", i=NT, h=H)).then_inc(*read("av"))
                for c in range(NT):
                    a.wait_ge(*bank_read(f"vg{c}", b))
                a.wait_ge(*gnv.before(b))
                a.activation(th[:], gin[:], ACT.Tanh, scale=0.5).then_inc(th_done.sem, 1)
                a.wait_ge(*gnp.before(b))
                for g in range(G):
                    a.wait_ge(*bank_full(f"U{g}", b))
                    a.copy(U[:, :, g * HG:(g + 1) * HG, :],
                                 bankof(f"U{g}")[:, 0:NT * HG * DV1].rearrange("p (c m v) -> p c m v", c=NT, v=DV1)).then_inc(*read(f"U{g}"))
                for k in range(2):
                    a.wait_ge(*bank_full(f"yT{k}", b))
                    a.copy(yT[:, k, :], bankof(f"yT{k}")).then_inc(*read(f"yT{k}"))
                a.wait_ge(*bank_full("mT", b))
                a.wait_ge(*m_spilled.before(b))
                a.mul(mTs[:], bankof("mT")[0:H, :], -1.0).then_inc(*read("mT"))
                for g in range(G):
                    for j in range(NT):
                        n = g * NT + j
                        if n >= 2:
                            g2, j2 = divmod(n - 2, NT)
                            if j2 == NT - 1:
                                a.wait_ge(*bank_full(f"O{g2}", b))
                            else:
                                a.wait_ge(*pv_done.count(b, g2 * (NT - 1) + j2 + 1))
                        for m in range(HG):
                            use = f"sc{g}{j}{m}"
                            a.wait_ge(*bank_full(use, b))
                            a.activation(PT[:, (j % 2) * HG + m, :], bankof(use), ACT.Exp).then_inc(*read(use))
                        if j == 0 and g > 0:
                            attention_sums(g - 1, b)
                attention_sums(G - 1, b)
                a.wait_ge(*bank_full("ctxT", b))
                a.copy(ctxT[:], bankof("ctxT")).then_inc(*read("ctxT"))
                a.wait_ge(*bank_read("xp", b))
                a.wait_ge(*h2_done.before(b))
                for i in range(NT):
                    a.activation(h2[:, i, :], X1[:, i, :], ACT.Square,
                                 accum_out=rs2[:, 0, i:i + 1]).then_inc(sq2_done.sem, 1)
                a.wait_ge(*bank_full("h2T", b))
                a.activation(h2T[:], bankof("h2T"), ACT.Identity, scale=colb[:, 5:6]).then_inc(*read("h2T"))
                a.wait_ge(*bank_read("lg", b))
                a.activation(lg[:, 1, :, :], lg[:, 0, :, :], ACT.Exp).then_inc(lga.sem, 1)
                a.wait_ge(*lgv.count(b, 6))
                a.activation(rt[:, 4, :], rt[:, 3, :], ACT.Exp).then_inc(lga.sem, 1)
                for u in range(UNITS):
                    if u == 2:
                        a.wait_ge(*bank_full("wT", b))
                        a.wait_ge(*w_spilled.before(b))
                        a.copy(wTs[:], bankof("wT")[0:E, :]).then_inc(*read("wT"))
                    a.wait_ge(*bank_full(f"ga{u}", b))
                    if u >= 3:
                        a.wait_ge(*down_done.count(b, u - 2))
                    a.activation(hid[:, u % 3, :], bankof(f"ga{u}"), ACT.Tanh, scale=0.5).then_inc(th2.sem, 1)
                a.wait_ge(*bank_full("moe", b))
                a.copy(moT[:], bankof("moe")).then_inc(*read("moe"))
                a.wait_ge(*bank_read("mo", b))
                a.activation(tY[:], Y[:], ACT.Tanh, scale=0.5).then_inc(tY_done.sem, 1)
            batch(0)
            with a.Fori(1, B) as b:
                batch(b)

        @block.gpsimd
        def _(p):
            p.wait_ge(inited.sem, 9)
            p.wait_ge(loaded.sem, 16 * n_loads[0])
            def batch(b):
                half4 = neghalf[:, 0:NT]
                p.wait_ge(*mv_done.count(b, NT))
                p.wait_ge(*xn_done.before(b))
                p.wait_ge(*hn_done.before(b))
                var = mv[:, :, 1]
                p.tensor_tensor(lnc[:, 0, :], var, consts[:, 0, :], ALU.add).then_inc(lnf.sem, 1)
                p.wait_ge(*lnf.count(b, 1))
                p.tensor_tensor(lnc[:, 1, :], lnc[:, 0, :], half4, ALU.pow).then_inc(lnf.sem, 1)
                p.wait_ge(*lnf.count(b, 2))
                p.tensor_tensor(lnc[:, 2, :], lnc[:, 1, :], var, ALU.mult).then_inc(lnf.sem, 1)
                p.wait_ge(*lnf.count(b, 3))
                p.tensor_tensor(lnc[:, 3, :], lnc[:, 2, :], lnc[:, 1, :], ALU.mult).then_inc(lnf.sem, 1)
                p.wait_ge(*lnf.count(b, 4))
                p.tensor_tensor(lnc[:, 3, :], lnc[:, 3, :], consts[:, 1, :], ALU.add).then_inc(lnf.sem, 1)
                p.wait_ge(*lnf.count(b, 5))
                p.tensor_tensor(lnc[:, 4, :], lnc[:, 3, :], half4, ALU.pow).then_inc(lnf.sem, 1)
                p.wait_ge(*lnf.count(b, 6))
                p.tensor_tensor(lnc[:, 5, :], lnc[:, 4, :], lnc[:, 1, :], ALU.mult).then_inc(lnf.sem, 1)
                p.wait_ge(*lnf.count(b, 7))
                p.wait_ge(*spilled.before(b))
                p.wait_ge(*qd_done.before(b))
                p.wait_ge(*filled[BANK["kT"]].before(b))
                p.wait_ge(*bank_read("rq", b))
                p.wait_ge(*bank_read("rqs", b))
                p.tensor_tensor(qr[:], rot[:, 0, :], rot[:, 1, :], ALU.add).then_inc(qk_done.sem, 1)
                p.wait_ge(*bank_read("rk", b))
                p.wait_ge(*bank_read("rks", b))
                p.tensor_tensor(rot[:, 2, :], rot[:, 2, :], rot[:, 3, :], ALU.add).then_inc(lnf.sem, 1)
                p.wait_ge(*lnf.count(b, 8))
                p.tensor_tensor(kr[:], rot[:, 2, :], consts[:, 3, 0:1].to_broadcast([P, S]), ALU.mult).then_inc(qk_done.sem, 1)
                p.wait_ge(*qk_done.count(b, 1))
                p.wait_ge(*drained[BANK["U3"]].before(b))
                p.tensor_tensor(qd[:], qr[:].rearrange("p (i s) -> p i s", i=NT),
                                qdec[:].unsqueeze(1).to_broadcast([P, NT, P]), ALU.mult).then_inc(qd_done.sem, 1)
                hv = "p c (h v) -> p c h v"
                p.wait_ge(*gnv.count(b, 3))
                p.wait_ge(*gs_done.count(b, 1))
                p.tensor_tensor(th[:].rearrange(hv, v=DV), U[:, :, :, 0:DV],
                                gn[:, 0, :].rearrange("p (c h) -> p c h", h=H).unsqueeze(3).to_broadcast([P, NT, H, DV]),
                                ALU.subtract).then_inc(gnp.sem, 1)
                p.wait_ge(*gnp.count(b, 1))
                p.wait_ge(*drained[BANK["yT1"]].before(b))
                p.tensor_tensor(sq[:], th[:], th[:], ALU.mult).then_inc(gnp.sem, 1)
                p.wait_ge(*gnv.count(b, 7))
                p.tensor_tensor(gn[:, 5, :], gn[:, 4, :], neghalf[:, 0:NT * H], ALU.pow).then_inc(gnp.sem, 1)
                p.wait_ge(*sq2_done.count(b, NT))
                p.tensor_tensor(rs2[:, 1, :], rs2[:, 0, :], consts[:, 2, :], ALU.mult).then_inc(rs2_done.sem, 1)
                p.wait_ge(*rs2_done.count(b, 1))
                p.tensor_tensor(rs2[:, 3, :], rs2[:, 1, :], consts[:, 1, :], ALU.add).then_inc(rs2_done.sem, 1)
                p.wait_ge(*rs2_done.count(b, 2))
                p.tensor_tensor(rs2[:, 2, :], rs2[:, 3, :], half4, ALU.pow).then_inc(rs2_done.sem, 1)
                p.wait_ge(*w_bcast.count(b, 16))
                for u in range(NF, UNITS):
                    p.wait_ge(*bank_read(f"up{u}", b))
                    t = hid[:, u % 3, :]
                    p.tensor_tensor(t, t, wbc[:, u // NF - 1, :], ALU.mult).then_inc(hidw.sem, 1)
            batch(0)
            with p.Fori(1, B) as b:
                batch(b)



_OUT = (B, S, D)


def kernel(**inputs):
    import concourse.bacc as _bacc
    from concourse.bass_utils import run_bass_kernel_spmd as _run

    def arr(name):
        return np.ascontiguousarray(inputs[name])

    swap = np.arange(D) ^ 1
    data = {
        "x": arr("L0_attn_x"),
        "Wq": arr("L0_attn_Wq"), "Wq_swapped": np.ascontiguousarray(arr("L0_attn_Wq")[:, swap]),
        "Wk": arr("L0_attn_Wk"), "Wk_swapped": np.ascontiguousarray(arr("L0_attn_Wk")[:, swap]),
        "Wv": arr("L0_attn_Wv"), "Wg": arr("L0_attn_Wg"), "Wo": arr("L0_attn_Wo"),
        "bv": arr("L0_attn_bv"), "bg": arr("L0_attn_bg"), "bo": arr("L0_attn_bo"),
        "columns": np.ascontiguousarray(np.stack(
            [arr("L0_attn_bq"), arr("L0_attn_bq")[swap], arr("L0_attn_bk"), arr("L0_attn_bk")[swap],
             arr("L0_ffn_norm1_w"), arr("L0_ffn_norm2_w")], axis=1)),
    }
    for name in ("wq", "wk", "wv", "wo", "router_w", "sh_gate", "sh_up", "sh_down", "e_gate", "e_up", "e_down"):
        data[name] = arr("L0_ffn_" + name)
    tables = {n: np.ascontiguousarray(t, dtype=np.float32) for n, t in shape_tables().items()}

    nc = _bacc.Bacc("TRN2", target_bir_lowering=False, num_devices=1)
    feed, ins, tabs = {}, {}, {}
    for group, made, prefix in ((data, ins, "in_"), (tables, tabs, "tab_")):
        for name, a in group.items():
            feed[prefix + name] = a
            made[name] = nc.dram_tensor(prefix + name, a.shape, mybir.dt.from_np(a.dtype), kind="ExternalInput").ap()
    out = nc.dram_tensor("out", _OUT, F32, kind="ExternalOutput").ap()
    build(nc, ins, tabs, out)
    r = _run(nc, [feed], core_ids=[0])
    return r.results[0]["out"]
```

```python
from contextlib import ExitStack

import numpy as np

import concourse.bass as bass
from concourse import mybir

ALU = mybir.AluOpType
ACT = mybir.ActivationFunctionType
F32 = mybir.dt.float32
F32R = mybir.dt.float32r
U32 = mybir.dt.uint32
AX_X = mybir.AxisListType.X

P = 128
B, S, D = 16, 512, 128
NT = S // P
H = 16
DK = D // H
DV = 2 * D // H
G = 4
HG = H // G
SLOT = 32
E = 8
FF = 256
NF = FF // P
UNITS = (E + 1) * NF
DV1 = DV + 1
DK1 = DK + 1
ROWS = 3 * DK
MROWS = ROWS + 2
U0 = UNITS - H
WB = 2
LN_EPS, RMS_EPS, GN_EPS = 1e-5, 1e-6, 1e-5


def shape_tables():
    f = np.float32
    angle = np.repeat((1.0 / 10000.0 ** np.linspace(0.0, 1.0, DK // 2)).astype(f), 2)
    arg = (np.arange(S, dtype=f)[:, None] * angle[None, :]).astype(f).astype(np.float64)
    sign = np.where(np.arange(DK) % 2 == 0, -1.0, 1.0)
    cos = np.tile(np.cos(arg).T, (H, 1)).astype(f)
    sin = np.tile((np.sin(arg) * sign).T, (H, 1)).astype(f)
    decay = np.log1p(-(2.0 ** (-5.0 - np.arange(H))))
    i = np.arange(P)
    diff = i[None, :] - i[:, None]
    mask = np.where(diff[:, None, :] >= 0, np.exp(decay[None, :, None] * np.maximum(diff, 0)[:, None, :]), 0.0)
    qdec = np.repeat(np.exp(decay[:, None] * (i[None, :] + 1)), DK, axis=0)
    kdec = np.repeat(np.exp(decay[None, :] * (P - 1 - i[:, None])), DK, axis=1)
    cdec = np.repeat(np.exp(decay * P), DK)[:, None]
    bd = (np.arange(D)[:, None] // DK == np.arange(H * DV1)[None, :] // DV1)
    a = np.arange(S)
    sums = -np.expm1(decay[None, :] * (a[:, None] + 1)) / -np.expm1(decay)[None, :]
    nrm = np.sqrt(sums).reshape(NT, P, H).transpose(1, 0, 2).reshape(P, NT * H)
    return {
        "cos": cos, "sin": sin, "mask": mask.reshape(P, H * P), "qdec": qdec, "kdec": kdec, "cdec": cdec,
        "bd": bd, "nrm": nrm, "ident": np.eye(P), "iota": np.tile(np.arange(E), (P, NT)),
    }


class Signal:

    def __init__(self, sem, per):
        self.sem, self.per = sem, per

    def at(self, b, k):
        return b * self.per + k

    def count(self, b, k):
        return self.sem, self.at(b, k)

    def before(self, b):
        return self.sem, self.at(b, 0)


def bank_uses():
    front = ["xnT", "hT", "rq", "rqs", "rk", "rks", "aq", "ak"] + [f"vg{c}" for c in range(NT)]
    front += ["kT"] + [f"st{c}" for c in range(NT - 1)]
    uses = [(n, i % 2) for i, n in enumerate(front)]
    for g in range(G):
        uses += [(f"rs{g}{m}", 0) for m in range(HG)]
        uses += [(f"U{g}", 1)]
    uses += [("yT0", 0), ("yT1", 1), ("sp", 0)]
    uses += [(f"mx{h}_{i}", i % 2) for h in range(H) for i in range(NT)]
    uses += [("av", 1), ("mT", 0)]
    for g in range(G):
        uses += [(f"O{g}", 4)]
        for j in range(NT):
            uses += [(f"sc{g}{j}{m}", 2 + m % 2) for m in range(HG)]
            if j == 1 and g:
                uses += [(f"OT{g - 1}", 2)]
    uses += [(f"OT{G - 1}", 2), ("ctxT", 3), ("xp", 2), ("h2T", 3), ("lg", 2), ("wT", 3)]
    for u in range(UNITS):
        uses += [(f"ga{u}", 5), (f"up{u}", 6)]
    uses += [("moe", 7), ("mo", 5)]
    bank, index, count = {}, {}, [0] * 8
    for name, k in uses:
        bank[name], index[name] = k, count[k]
        count[k] += 1
    return bank, index, count


def build(nc, ins, tabs, out):
    with ExitStack() as ctx:
        def sb(name, shape, dt=F32):
            return ctx.enter_context(nc.sbuf_tensor(name, shape, dt))

        def sig(name, per):
            return Signal(ctx.enter_context(nc.semaphore(name)), per)

        BANK, INDEX, COUNT = bank_uses()
        psum = ctx.enter_context(nc.psum_tensor("psum", [P, 8, 512], F32))
        filled = [sig(f"bank{k}_filled", COUNT[k]) for k in range(8)]
        drained = [sig(f"bank{k}_drained", COUNT[k]) for k in range(8)]

        def bankof(use):
            return psum[:, BANK[use], :]

        ident = sb("ident", [P, P])
        cos, sin = sb("cos", [P, S]), sb("sin", [P, S])
        mask = sb("mask", [P, H, P])
        qdec, kdec, cdec = sb("qdec", [P, P]), sb("kdec", [P, D]), sb("cdec", [P, 1])
        bd = sb("bd", [P, H * DV1])
        nrm = sb("nrm", [P, NT * H])
        iota = sb("iota", [P, NT, E])
        w_rq, w_rqs, w_rk, w_rks = (sb(n, [P, D]) for n in ("w_rq", "w_rqs", "w_rk", "w_rks"))
        w_vg = sb("w_vg", [P, 4 * D])
        w_ro = sb("w_ro", [P, 2, D])
        w_aq, w_ak, w_av, w_ao = (sb(n, [P, D]) for n in ("w_aq", "w_ak", "w_av", "w_ao"))
        w_rt = sb("w_rt", [P, E])
        w_rt_hi, w_rt_lo = sb("w_rt_hi", [P, E], F32R), sb("w_rt_lo", [P, E], F32R)
        w_gate_hi, w_gate_lo = (sb(n, [P, E + 1, FF], F32R) for n in ("w_gate_hi", "w_gate_lo"))
        w_up_hi, w_up_lo = (sb(n, [P, E + 1, FF], F32R) for n in ("w_up_hi", "w_up_lo"))
        w_down = sb("w_down", [P, UNITS, D])
        colb = sb("colb", [P, 6])
        b_vg = sb("b_vg", [P, 4 * D])
        b_o = sb("b_o", [P, D])
        neghalf = sb("neghalf", [P, 64])
        consts = sb("consts", [P, 4, NT])
        x_in = sb("x_in", [P, NT, D])
        stats = sb("stats", [P, NT, 6])
        mv = sb("mv", [P, NT, 2])
        lnc = sb("lnc", [P, 6, NT])
        xn, hn = sb("xn", [P, NT, D]), sb("hn", [P, NT, D])
        xnT, hT = sb("xnT", [P, S]), sb("hT", [P, S])
        rot = sb("rot", [P, 4, S])
        kd = rot[:, 2, :].rearrange("p (i d) -> p i d", i=NT)
        qd = rot[:, 3, :].rearrange("p (i s) -> p i s", i=NT)
        yT = rot[:, 0:2, :]
        qr, kr = sb("qr", [P, S]), sb("kr", [P, S])
        aq_hi, aq_lo, ak_hi, ak_lo = (sb(n, [P, S], F32R) for n in ("aq_hi", "aq_lo", "ak_hi", "ak_lo"))
        rqp, rkp = sb("rqp", [P, G, S]), sb("rkp", [P, G, S])
        aqp, akp = sb("aqp", [P, G, S], F32R), sb("akp", [P, G, S], F32R)
        state = sb("state", [P, NT - 1, H * DV1])
        vr = sb("vr", [P, NT, H, DV1])
        arena = sb("arena", [P, 2 * 512 + NT * H * DV1 + 2 * NT * 2 * D])
        rsc = arena[:, 0:1024].rearrange("p (a n) -> p a n", a=2)
        U = arena[:, 1024:1024 + NT * H * DV1].rearrange("p (c h v) -> p c h v", c=NT, h=H)
        sq = arena[:, 1024:2048].rearrange("p (c n) -> p c n", c=NT)
        o_th = 1024 + NT * H * DV1
        th = arena[:, o_th:o_th + 1024].rearrange("p (c n) -> p c n", c=NT)
        gin = arena[:, o_th + 1024:o_th + 2048].rearrange("p (c n) -> p c n", c=NT)
        PT = arena[:, 0:4096].rearrange("p (a n) -> p a n", a=8)
        gn = sb("gn", [P, 6, NT * H])
        s_out = sb("s_out", [P, NT, D])
        mx = sb("mx", [P, NT, H])
        m_hi = sb("m_hi", [P, NT, H], F32R)
        m2 = sb("m2", [P, NT, 2, H])
        rows_T = sb("rows_T", [2 * SLOT, S])
        mTs = rows_T[0:2 * H, :].bitcast(F32R)
        aqx, akx = sb("aqx", [P, G, S], F32R), sb("akx", [P, G, S], F32R)
        vt = sb("vt", [P, NT, H, DK1])
        Os = qr
        rec = sb("rec", [P, NT, HG])
        ctxt = kr[:].rearrange("p (i d) -> p i d", i=NT)
        ctxT = xnT
        xn_b = sb("xn_b", [P, NT, D])
        X1 = sb("X1", [P, NT, D])
        rs2 = sb("rs2", [P, 4, NT])
        h2 = hn
        h2_hi, h2_lo = sb("h2_hi", [P, S], F32R), sb("h2_lo", [P, S], F32R)
        lg = sb("lg", [P, 4, NT, E])
        rt = sb("rt", [P, 8, NT])
        top = sb("top", [P, NT, 8])
        topi = sb("topi", [P, NT, 8], U32)
        topf = sb("topf", [P, NT, 8])
        wTs = rows_T[SLOT:SLOT + E, :]
        wbc = sb("wbc", [P, WB, S])
        hid = sb("hid", [P, 3, S])
        x_res, s_res = sb("x_res", [P, NT, D]), sb("s_res", [P, NT, D])
        Y, tY = sb("Y", [P, NT, D]), sb("tY", [P, NT, D])
        moT = tY[:].rearrange("p i d -> p (i d)")
        d_rq, d_rk = (nc.dram_tensor(n, [P, S], F32, kind="Internal").ap() for n in ("d_rq", "d_rk"))
        d_aq, d_ak = (nc.dram_tensor(n, [2, P, S], F32, kind="Internal").ap() for n in ("d_aq", "d_ak"))
        d_m = nc.dram_tensor("d_m", [2 * H, S], F32, kind="Internal").ap()
        d_w = nc.dram_tensor("d_w", [E, S], F32, kind="Internal").ap()
        d_xn = nc.dram_tensor("d_xn", [B, P, NT * D], F32, kind="Internal").ap()
        d_s = nc.dram_tensor("d_s", [B, P, NT * D], F32, kind="Internal").ap()

        loaded, split_ld = sig("weights_loaded", 0), sig("weights_to_split_loaded", 0)
        scaled = sig("weights_scaled", 0)
        split = sig("weights_split", 0)
        inited = sig("constants_written", 0)
        x_ld, x_res_ld, s_res_ld = sig("x_loaded", 16), sig("x_res_loaded", 16), sig("s_res_loaded", 16)
        mv_done = sig("mean_var_done", NT)
        lnf = sig("norm_factors_step", 8)
        xn_done, hn_done = sig("xn_done", NT), sig("hn_done", NT)
        xn_spilled, xn_b_ld = sig("xn_spilled", 16), sig("xn_reloaded", 16)
        s_spilled = sig("retention_out_spilled", 16)
        qk_done = sig("rotary_sums_done", 2)
        ahi_done = sig("attention_qk_high_done", 2)
        spilled_r, spilled_a = sig("retention_qk_spilled", 32), sig("attention_qk_spilled", 64)
        slot_r, slot_a = sig("retention_qk_slotted", 16 * 2 * HG), sig("attention_qk_slotted", 16 * 6 * HG)
        qd_done = sig("decayed_q_done", 1)
        vr_done = sig("retention_v_done", NT)
        th_done, gs_done = sig("gate_tanh_done", 1), sig("gate_silu_done", 1)
        st_done = sig("state_step_done", NT - 2)
        pv_ret = sig("retention_sums_step", G * (HG - 1))
        gnp = sig("group_norm_pool_step", 3)
        gnv = sig("group_norm_vector_step", 9)
        m_done = sig("neg_max_step", 3)
        m_spilled, m_slotted = sig("neg_max_spilled", 16), sig("neg_max_slotted", 16 * HG)
        x_copied = sig("slots_copied", 32)
        pv_done = sig("pv_step_done", G * (NT - 1))
        rec_done = sig("softmax_recip_done", G)
        sq2_done = sig("residual_squares_done", NT)
        rs2_done = sig("rms2_factor_step", 3)
        h2_done = sig("h2_done", NT)
        h2hi_done = sig("h2_high_done", 1)
        lgv = sig("router_vector_step", 12)
        lgw = sig("router_weights_step", 2)
        lga = sig("router_exp_step", 2)
        w_spilled = sig("combine_spilled", 16)
        w_bcast = [sig(f"combine_broadcast_to_slot{k}", 16 * E // WB) for k in range(WB)]
        th2 = sig("expert_tanh_done", UNITS)
        hidw = sig("expert_hidden_weighted", UNITS - NF)
        down_done = sig("down_step_done", UNITS - 1)
        Yv, tY_done = sig("final_vector_step", 3), sig("final_tanh_done", 1)
        stored = sig("output_stored", 16)

        def bank_free(use, b):
            k = BANK[use]
            return drained[k].sem, drained[k].at(b, INDEX[use])

        def bank_full(use, b):
            k = BANK[use]
            return filled[k].sem, filled[k].at(b, INDEX[use] + 1)

        def bank_read(use, b):
            k = BANK[use]
            return drained[k].sem, drained[k].at(b, INDEX[use] + 1)

        def full(use):
            return filled[BANK[use]].sem, 1

        def read(use):
            return drained[BANK[use]].sem, 1

        def iterations(eng, iteration):
            iteration(0, True, False, False)
            iteration(1, True, True, False)
            with eng.Fori(2, B - 1) as i:
                iteration(i, True, True, True)
            iteration(B - 1, True, True, True, last=True)
            iteration(B, False, True, True)
            iteration(B + 1, False, False, True)

        n_loads = [0]
        flat = "p i n -> p (i n)"
        block = ctx.enter_context(nc.Block())

        @block.sync
        def _(sp):
            def ld(dst, src):
                sp.dma_start(dst, src).then_inc(loaded.sem, 16)
                n_loads[0] += 1

            def x_tiles(b):
                return ins["x"][bass.ds(b, 1)].rearrange("o (i p) d -> p (o i) d", p=P)

            sp.dma_start(x_in[:], x_tiles(0)).then_inc(x_ld.sem, 16)
            ld(ident[:], tabs["ident"])
            for dst, name in ((w_rq, "Wq"), (w_rqs, "Wq_swapped"), (w_rk, "Wk"), (w_rks, "Wk_swapped")):
                ld(dst[:], ins[name])
            for dst, name in ((w_aq, "wq"), (w_ak, "wk"), (w_av, "wv"), (w_ao, "wo"), (w_rt, "router_w")):
                ld(dst[:], ins[name])
            ld(colb[:], ins["columns"])
            for dst, name in ((cos, "cos"), (sin, "sin"), (qdec, "qdec"), (kdec, "kdec"), (cdec, "cdec"), (bd, "bd"),
                              (nrm, "nrm")):
                ld(dst[:], tabs[name])
            ld(w_vg[:, 0:2 * D], ins["Wv"])
            ld(w_vg[:, 2 * D:4 * D], ins["Wg"])
            ld(b_vg[:, 0:2 * D], bass.AP(ins["bv"].tensor, 0, [[0, P], [1, 2 * D]]))
            ld(b_vg[:, 2 * D:4 * D], bass.AP(ins["bg"].tensor, 0, [[0, P], [1, 2 * D]]))
            ld(b_o[:], bass.AP(ins["bo"].tensor, 0, [[0, P], [1, D]]))
            ld(w_ro[:], ins["Wo"].rearrange("(a p) n -> p a n", p=P))
            ld(mask[:], tabs["mask"].rearrange("p (h s) -> p h s", h=H))
            ld(iota[:], tabs["iota"].rearrange("p (i e) -> p i e", e=E))
            ld(w_down[:, 0:NF, :], ins["sh_down"].rearrange("(a p) n -> p a n", p=P))
            ld(w_down[:, NF:, :], ins["e_down"].rearrange("e (a p) n -> p (e a) n", p=P))
            for n, (sh, ex) in enumerate((("sh_gate", "e_gate"), ("sh_up", "e_up"))):
                raw = arena[:, 0:(E + 1) * FF].rearrange("p (e f) -> p e f", f=FF)
                if n:
                    sp.wait_ge(split.sem, 2)
                sp.dma_start(raw[:, 0, :], ins[sh]).then_inc(split_ld.sem, 16)
                sp.dma_start(raw[:, 1:, :], ins[ex].rearrange("e p f -> p e f")).then_inc(split_ld.sem, 16)

            def iteration(i, A, Bs, C, last=False):
                b, c = i - 1, i - 2
                tiles = "o p (i d) -> p (o i) d"
                if A:
                    xn_to, s_to = (d[bass.ds(i, 1)].rearrange("o p n -> p (o n)") for d in (d_xn, d_s))
                    x_next = None if last else x_tiles(i + 1)
                if Bs:
                    xn_from = d_xn[bass.ds(b, 1)].rearrange(tiles, d=D)
                if C:
                    s_from, x_again = d_s[bass.ds(c, 1)].rearrange(tiles, d=D), x_tiles(c)
                    out_to = out[bass.ds(c, 1)].rearrange("o (i p) d -> p (o i) d", p=P)
                if A:
                    sp.wait_ge(*xn_done.count(i, NT))
                    sp.dma_start(xn_to, xn[:].rearrange(flat)).then_inc(xn_spilled.sem, 16)
                    for k, (s, dst) in enumerate(((qr, d_rq), (kr, d_rk))):
                        sp.wait_ge(*qk_done.count(i, k + 1))
                        sp.dma_start(dst, s[:]).then_inc(spilled_r.sem, 16)
                    for k, (hi, lo, dst) in enumerate(((aq_hi, aq_lo, d_aq), (ak_hi, ak_lo, d_ak))):
                        sp.wait_ge(*bank_read(("aq", "ak")[k], i))
                        sp.dma_start(dst[0], hi[:].bitcast(F32)).then_inc(spilled_a.sem, 16)
                        sp.dma_start(dst[1], lo[:].bitcast(F32)).then_inc(spilled_a.sem, 16)
                    sp.wait_ge(*spilled_r.count(i, 32))
                    sp.wait_ge(*filled[BANK["U3"]].before(i))
                    for src, dst in ((d_rq, rqp), (d_rk, rkp)):
                        for m in range(HG):
                            sp.dma_start(dst[SLOT * m:SLOT * m + DK, :, :],
                                         src.rearrange("(g m d) s -> m d g s", g=G, m=HG)[m]).then_inc(slot_r.sem, 16)
                    sp.wait_ge(*spilled_a.count(i, 64))
                    sp.wait_ge(*x_copied.before(i))
                    for src, dst, parts in ((d_aq, aqp, (0, 0, 1)), (d_ak, akp, (0, 1, 0))):
                        for m in range(HG):
                            for k, part in enumerate(parts):
                                r = SLOT * m + k * DK
                                sp.dma_start(dst[r:r + DK, :, :].bitcast(F32),
                                             src[part].rearrange("(g m d) s -> m d g s", g=G, m=HG)[m]
                                             ).then_inc(slot_a.sem, 16)
                    if not last:
                        sp.wait_ge(*hn_done.count(i, NT))
                        sp.dma_start(x_in[:], x_next).then_inc(x_ld.sem, 16)
                if Bs:
                    sp.wait_ge(*drained[BANK["xp"]].before(b))
                    sp.wait_ge(*xn_spilled.count(b, 16))
                    sp.dma_start(xn_b[:], xn_from).then_inc(xn_b_ld.sem, 16)
                if C:
                    sp.wait_ge(*Yv.before(c))
                    sp.wait_ge(*s_spilled.count(c, 16))
                    sp.dma_start(s_res[:], s_from).then_inc(s_res_ld.sem, 16)
                    sp.dma_start(x_res[:], x_again).then_inc(x_res_ld.sem, 16)
                if A:
                    sp.wait_ge(*bank_read("sp", i))
                    sp.dma_start(s_to, s_out[:].rearrange(flat)).then_inc(s_spilled.sem, 16)
                    if Bs:
                        sp.wait_ge(*bank_full("sc332", b))
                        sp.wait_ge(*bank_full("sc333", b))
                    sp.wait_ge(*slot_a.count(i, slot_a.per))
                    sp.dma_start(aqx[:].bitcast(F32), aqp[:].bitcast(F32)).then_inc(x_copied.sem, 16)
                    sp.dma_start(akx[:].bitcast(F32), akp[:].bitcast(F32)).then_inc(x_copied.sem, 16)
                    sp.wait_ge(*bank_read("mT", i))
                    sp.dma_start(d_m, rows_T[0:2 * H, :]).then_inc(m_spilled.sem, 16)
                    sp.wait_ge(*m_spilled.count(i, 16))
                    sp.wait_ge(*x_copied.count(i, 32))
                    for m in range(HG):
                        sp.dma_start(aqx[SLOT * m + ROWS:SLOT * m + MROWS, :, :].bitcast(F32),
                                     d_m.rearrange("(a g m) s -> m a g s", a=2, m=HG)[m]).then_inc(m_slotted.sem, 16)
                if C:
                    sp.wait_ge(*Yv.count(c, 3))
                    sp.dma_start(out_to, Y[:]).then_inc(stored.sem, 16)
                if Bs:
                    sp.wait_ge(*bank_read("wT", b))
                    if C:
                        for k in range(WB):
                            sp.wait_ge(*w_bcast[k].count(c, w_bcast[k].per))
                    sp.dma_start(d_w, wTs).then_inc(w_spilled.sem, 16)

            iterations(sp, iteration)
            sp.wait_ge(stored.sem, 16 * B)

        @block.tensor
        def _(pe):
            pe.wait_ge(loaded.sem, 16 * n_loads[0])
            pe.wait_ge(scaled.sem, 2)
            pe.wait_ge(inited.sem, 12)

            def mm(o, l, r, start=True, stop=True, **kw):
                return pe.matmul(o, l, r, start=start, stop=stop, **kw)

            def four(use, b, src, rows=P):
                pe.wait_ge(*bank_free(use, b))
                for i in range(NT):
                    ins_ = pe.transpose(bankof(use)[0:rows, i * P:(i + 1) * P], src(i), ident[:])
                ins_.then_inc(*full(use))

            def front(b):
                pe.wait_ge(*xn_done.count(b, NT))
                four("xnT", b, lambda i: xn[:, i, :])
                pe.wait_ge(*hn_done.count(b, NT))
                four("hT", b, lambda i: hn[:, i, :])
                pe.wait_ge(*bank_read("xnT", b))
                for use, w in (("rq", w_rq), ("rqs", w_rqs), ("rk", w_rk), ("rks", w_rks)):
                    pe.wait_ge(*bank_free(use, b))
                    mm(bankof(use), w[:], xnT[:]).then_inc(*full(use))
                pe.wait_ge(*bank_read("hT", b))
                for use, w in (("aq", w_aq), ("ak", w_ak)):
                    pe.wait_ge(*bank_free(use, b))
                    mm(bankof(use), w[:], hT[:]).then_inc(*full(use))
                for c in range(NT):
                    use = f"vg{c}"
                    pe.wait_ge(*bank_free(use, b))
                    mm(bankof(use), xnT[:, c * P:(c + 1) * P], w_vg[:]).then_inc(*full(use))

            def states(b):
                pe.wait_ge(*qk_done.count(b, 2))
                four("kT", b, lambda i: kr[:, i * P:(i + 1) * P])
                pe.wait_ge(*bank_read("kT", b))
                for c in range(NT - 1):
                    use = f"st{c}"
                    pe.wait_ge(*bank_free(use, b))
                    pe.wait_ge(*vr_done.count(b, c + 1))
                    mm(bankof(use)[:, 0:H * DV1], kd[:, c, :],
                       vr[:, c, :, :].rearrange("p h v -> p (h v)")).then_inc(*full(use))
                pe.wait_ge(*slot_r.count(b, slot_r.per))
                pe.wait_ge(*bank_read(f"st{NT - 2}", b))
                pe.wait_ge(*st_done.count(b, st_done.per))
                pe.wait_ge(*vr_done.count(b, NT))
                pe.wait_ge(*qd_done.count(b, 1))

            def ret_scores(b, g, m):
                use = f"rs{g}{m}"
                pe.wait_ge(*bank_free(use, b))
                r = slice(SLOT * m, SLOT * m + DK)
                for c in range(NT):
                    ins_ = mm(bankof(use)[:, c * P:(c + 1) * P], rkp[r, g, c * P:(c + 1) * P],
                              rqp[r, g, c * P:(c + 1) * P])
                ins_.then_inc(*full(use))

            def ret_sums(b, g, m):
                use, w = f"U{g}", HG * DV1
                if m == 0:
                    pe.wait_ge(*bank_free(use, b))
                    for c in range(1, NT):
                        mm(bankof(use)[:, c * w:(c + 1) * w], qd[SLOT * g:SLOT * g + SLOT, c, :],
                           state[SLOT * g:SLOT * g + SLOT, c - 1, g * w:(g + 1) * w],
                           start=(c == 1), stop=False, skip_group_check=True)
                pe.wait_ge(*bank_read(f"rs{g}{m}", b))
                for c in range(NT):
                    ins_ = mm(bankof(use)[:, c * w + m * DV1:c * w + (m + 1) * DV1],
                              rsc[:, (g * HG + m) % 2, c * P:(c + 1) * P], vr[:, c, g * HG + m, :],
                              start=False, stop=(m == HG - 1), skip_group_check=True)
                if m == HG - 1:
                    ins_.then_inc(*full(use))
                else:
                    ins_.then_inc(pv_ret.sem, 1)

            def retention(b):
                steps = [(g, m) for g in range(G) for m in range(HG)]
                ret_scores(b, *steps[0])
                for n, (g, m) in enumerate(steps):
                    if n + 1 < len(steps):
                        ret_scores(b, *steps[n + 1])
                    ret_sums(b, g, m)

            def retention_out(b):
                pe.wait_ge(*gnv.count(b, gnv.per))
                for a in range(2):
                    four(f"yT{a}", b, lambda i: sq[:, i, a * D:(a + 1) * D])
                pe.wait_ge(*bank_free("sp", b))
                pe.wait_ge(*bank_read("yT0", b))
                pe.wait_ge(*bank_read("yT1", b))
                for i in range(NT):
                    for a in range(2):
                        ins_ = mm(bankof("sp")[:, i * D:(i + 1) * D], yT[:, a, i * P:(i + 1) * P], w_ro[:, a, :],
                                  start=(a == 0), stop=(a == 1))
                ins_.then_inc(*full("sp"))

            def max_scores(b, h, half):
                g, m = divmod(h, HG)
                r = slice(SLOT * m, SLOT * m + ROWS)
                for i in (2 * half, 2 * half + 1):
                    use = f"mx{h}_{i}"
                    pe.wait_ge(*bank_free(use, b))
                    mm(bankof(use), aqp[r, g, i * P:(i + 1) * P], akp[r, g, :]).then_inc(*full(use))

            def attention_v(b):
                pe.wait_ge(*bank_free("av", b))
                for i in range(NT):
                    ins_ = mm(bankof("av")[:, i * D:(i + 1) * D], hT[:, i * P:(i + 1) * P], w_av[:])
                ins_.then_inc(*full("av"))

            def maxima(b):
                pe.wait_ge(*m_done.count(b, 3))
                four("mT", b, lambda i: m2[:, i, :, :].rearrange("p a h -> p (a h)"), rows=2 * H)

            def att_scores(b, g, j, half):
                for m in (2 * half, 2 * half + 1):
                    use = f"sc{g}{j}{m}"
                    r = slice(SLOT * m, SLOT * m + MROWS)
                    pe.wait_ge(*bank_free(use, b))
                    mm(bankof(use), akx[r, g, j * P:(j + 1) * P], aqx[r, g, :]).then_inc(*full(use))

            def att_pv(b, g, j):
                if j == 0:
                    pe.wait_ge(*bank_free(f"O{g}", b))
                pe.wait_ge(*bank_read(f"sc{g}{j}2", b))
                pe.wait_ge(*bank_read(f"sc{g}{j}3", b))
                for m in range(HG):
                    ins_ = mm(bankof(f"O{g}")[SLOT * m:SLOT * m + DK1, :], vt[:, j, g * HG + m, :],
                              PT[:, (j % 2) * HG + m, :], start=(j == 0), stop=(j == NT - 1))
                if j == NT - 1:
                    ins_.then_inc(*full(f"O{g}"))
                else:
                    ins_.then_inc(pv_done.sem, 1)

            def att_out(b, g):
                pe.wait_ge(*bank_read(f"O{g}", b))
                four(f"OT{g}", b, lambda i: Os[:, i * P:(i + 1) * P])

            def residual(b):
                pe.wait_ge(*bank_read("ctxT", b))
                pe.wait_ge(*bank_free("xp", b))
                for i in range(NT):
                    ins_ = mm(bankof("xp")[:, i * D:(i + 1) * D], ctxT[:, i * P:(i + 1) * P], w_ao[:])
                ins_.then_inc(*full("xp"))

            def router(b):
                pe.wait_ge(*h2_done.count(b, NT))
                four("h2T", b, lambda i: h2[:, i, :])
                pe.wait_ge(*bank_read("h2T", b))
                pe.wait_ge(*bank_free("lg", b))
                for i in range(NT):
                    t = slice(i * P, (i + 1) * P)
                    o = bankof("lg")[:, i * E:(i + 1) * E]
                    mm(o, h2_hi[:, t], w_rt_hi[:], stop=False)
                    mm(o, h2_hi[:, t], w_rt_lo[:], start=False, stop=False)
                    ins_ = mm(o, h2_lo[:, t], w_rt_hi[:], start=False)
                ins_.then_inc(*full("lg"))

            def combine(b):
                pe.wait_ge(*lgv.count(b, lgv.per))
                four("wT", b, lambda i: lg[:, 3, i, :], rows=E)

            def hidden(b, u, use, hi, lo):
                e, f = divmod(u, NF)
                w = slice(f * P, (f + 1) * P)
                if u == 0:
                    pe.wait_ge(*bank_read("h2T", b))
                pe.wait_ge(*bank_free(use, b))
                mm(bankof(use), hi[:, e, w], h2_hi[:], stop=False)
                mm(bankof(use), hi[:, e, w], h2_lo[:], start=False, stop=False)
                mm(bankof(use), lo[:, e, w], h2_hi[:], start=False).then_inc(*full(use))

            def gate(b, u):
                hidden(b, u, f"ga{u}", w_gate_hi, w_gate_lo)

            def up(b, u):
                hidden(b, u, f"up{u}", w_up_hi, w_up_lo)

            def down(b, u):
                if u == 0:
                    pe.wait_ge(*bank_free("moe", b))
                if u < NF:
                    pe.wait_ge(*bank_read(f"up{u}", b))
                else:
                    pe.wait_ge(*hidw.count(b, u - NF + 1))
                ins_ = mm(bankof("moe"), w_down[:, u, :], hid[:, u % 3, :], start=(u == 0), stop=(u == UNITS - 1))
                if u == UNITS - 1:
                    ins_.then_inc(*full("moe"))
                else:
                    ins_.then_inc(down_done.sem, 1)

            def iteration(i, A, Bs, C, last=False):
                b, c = i - 1, i - 2
                if C:
                    for u in range(U0):
                        gate(c, u)
                        up(c, u)
                if A:
                    front(i)
                    states(i)
                    retention(i)
                    retention_out(i)
                    pe.wait_ge(*slot_a.count(i, slot_a.per))
                if Bs:
                    pe.wait_ge(*m_slotted.count(b, m_slotted.per))
                    pe.wait_ge(*bank_read("av", b))
                for n in range(H):
                    g, j = divmod(n, NT)
                    if Bs:
                        att_scores(b, g, j, 0)
                    if A:
                        max_scores(i, n, 0)
                    if C:
                        gate(c, n + U0)
                    if Bs:
                        att_scores(b, g, j, 1)
                    if A:
                        max_scores(i, n, 1)
                    if C:
                        up(c, n + U0)
                    if Bs:
                        if n:
                            att_pv(b, *divmod(n - 1, NT))
                        if j == 1 and g:
                            att_out(b, g - 1)
                    if C:
                        down(c, n)
                if Bs:
                    att_pv(b, G - 1, NT - 1)
                if C:
                    for u in range(H, UNITS):
                        down(c, u)
                if Bs:
                    att_out(b, G - 1)
                if A:
                    attention_v(i)
                    maxima(i)
                if C:
                    pe.wait_ge(*bank_read("moe", c))
                    four("mo", c, lambda i: moT[:, i * P:(i + 1) * P])
                if Bs:
                    pe.wait_ge(*bank_read(f"OT{G - 1}", b))
                    four("ctxT", b, lambda i: ctxt[:, i, :])
                    residual(b)
                    router(b)
                    combine(b)

            iterations(pe, iteration)

        @block.vector
        def _(v):
            v.memset(neghalf[:], -0.5).then_inc(inited.sem, 1)
            for n, value in enumerate((LN_EPS, RMS_EPS, 1.0 / D, float(DK) ** -0.5)):
                v.memset(consts[:, n, :], value).then_inc(inited.sem, 1)
            v.memset(vr[:, :, :, DV:DV1], 1.0).then_inc(inited.sem, 1)
            v.memset(vt[:, :, :, DK:DK1], 1.0).then_inc(inited.sem, 1)
            v.memset(akp[:].bitcast(F32), 1.0).then_inc(inited.sem, 1)
            v.memset(aqp[:].bitcast(F32), 1.0).then_inc(inited.sem, 1)
            v.memset(bankof("O0"), 0.0).then_inc(inited.sem, 1)
            v.wait_ge(loaded.sem, 16 * n_loads[0])
            v.tensor_scalar(w_down[:], w_down[:], 0.5, None, ALU.mult).then_inc(scaled.sem, 1)
            v.tensor_scalar(w_ro[:], w_ro[:], 0.5, None, ALU.mult).then_inc(scaled.sem, 1)
            v.tensor_copy(w_rt_hi[:], w_rt[:]).then_inc(inited.sem, 1)
            v.wait_ge(inited.sem, 11)
            v.tensor_tensor(w_rt_lo[:], w_rt[:], w_rt_hi[:].bitcast(F32), ALU.subtract).then_inc(inited.sem, 1)
            raw = arena[:, 0:(E + 1) * FF].rearrange("p (e f) -> p e f", f=FF)
            for n, (hi, lo) in enumerate(((w_gate_hi, w_gate_lo), (w_up_hi, w_up_lo))):
                v.wait_ge(split_ld.sem, 32 * (n + 1))
                v.tensor_copy(hi[:], raw).then_inc(split.sem, 1)
                v.wait_ge(split.sem, 2 * n + 1)
                v.tensor_tensor(lo[:], raw, hi[:].bitcast(F32), ALU.subtract).then_inc(split.sem, 1)
            v.wait_ge(inited.sem, 12)
            v.wait_ge(split.sem, 4)

            def norms(b):
                v.wait_ge(*lnf.before(b))
                v.wait_ge(*x_ld.count(b, 16))
                for i in range(NT):
                    v.bn_stats(stats[:, i, :], x_in[:, i, :])
                v.drain()
                for i in range(NT):
                    v.bn_aggr(mv[:, i, :], stats[:, i, :]).then_inc(mv_done.sem, 1)
                v.wait_ge(*lnf.count(b, 2))
                v.wait_ge(*filled[BANK["xnT"]].before(b))
                v.wait_ge(*xn_spilled.before(b))
                for i in range(NT):
                    v.tensor_scalar(xn[:, i, :], x_in[:, i, :], mv[:, i, 0:1], lnc[:, 1, i:i + 1],
                                    ALU.subtract, ALU.mult).then_inc(xn_done.sem, 1)
                v.wait_ge(*lnf.count(b, 7))
                v.wait_ge(*filled[BANK["hT"]].before(b))
                for i in range(NT):
                    v.tensor_scalar(hn[:, i, :], x_in[:, i, :], mv[:, i, 0:1], lnc[:, 5, i:i + 1],
                                    ALU.subtract, ALU.mult).then_inc(hn_done.sem, 1)

            def projections(b):
                v.wait_ge(*qk_done.before(b))
                for n, (use, tab) in enumerate((("rq", cos), ("rqs", sin), ("rk", cos), ("rks", sin))):
                    v.wait_ge(*bank_full(use, b))
                    v.scalar_tensor_tensor(rot[:, n, :], bankof(use), colb[:, n:n + 1], tab[:], ALU.add,
                                           ALU.mult).then_inc(*read(use))
                v.wait_ge(*spilled_a.before(b))
                for use, scale, hi, lo in (("aq", float(DK) ** -0.5, aq_hi, aq_lo), ("ak", 1.0, ak_hi, ak_lo)):
                    v.wait_ge(*ahi_done.count(b, 1 if use == "aq" else 2))
                    v.scalar_tensor_tensor(lo[:], bankof(use), scale, hi[:].bitcast(F32), ALU.mult,
                                           ALU.subtract).then_inc(*read(use))
                for c in range(NT):
                    use = f"vg{c}"
                    hv = "p (h v) -> p h v"
                    v.wait_ge(*bank_full(use, b))
                    v.tensor_tensor(vr[:, c, :, 0:DV], bankof(use)[:, 0:2 * D].rearrange(hv, h=H),
                                    b_vg[:, 0:2 * D].rearrange(hv, h=H), ALU.add).then_inc(vr_done.sem, 1)
                    v.tensor_tensor(gin[:, c, :], bankof(use)[:, 2 * D:4 * D], b_vg[:, 2 * D:4 * D],
                                    ALU.add).then_inc(*read(use))

            def states(b):
                v.wait_ge(*bank_full("kT", b))
                v.tensor_tensor(kd, bankof("kT").rearrange("p (i d) -> p i d", i=NT),
                                kdec[:].unsqueeze(1).to_broadcast([P, NT, D]), ALU.mult).then_inc(*read("kT"))
                for c in range(NT - 1):
                    use = f"st{c}"
                    v.wait_ge(*bank_full(use, b))
                    v.tensor_tensor(state[:, c, :], bankof(use)[:, 0:H * DV1], bd[:], ALU.mult).then_inc(*read(use))
                    if c > 0:
                        v.wait_ge(*bank_read(use, b))
                        if c > 1:
                            v.wait_ge(*st_done.count(b, c - 1))
                        v.scalar_tensor_tensor(state[:, c, :], state[:, c - 1, :], cdec[:, 0:1], state[:, c, :],
                                               ALU.mult, ALU.add).then_inc(st_done.sem, 1)

            def retention(b):
                cs = "p (c s) -> p c s"
                for g in range(G):
                    for m in range(HG):
                        n = g * HG + m
                        use = f"rs{g}{m}"
                        v.wait_ge(*bank_full(use, b))
                        if n >= 2:
                            g2, m2_ = divmod(n - 2, HG)
                            if m2_ == HG - 1:
                                v.wait_ge(*bank_full(f"U{g2}", b))
                            else:
                                v.wait_ge(*pv_ret.count(b, g2 * (HG - 1) + m2_ + 1))
                        v.tensor_tensor(rsc[:, n % 2, :].rearrange(cs, c=NT), bankof(use).rearrange(cs, c=NT),
                                        mask[:, n, :].unsqueeze(1).to_broadcast([P, NT, P]),
                                        ALU.mult).then_inc(*read(use))

            def group_norm(b):
                v.wait_ge(*th_done.count(b, 1))
                v.scalar_tensor_tensor(gin.rearrange(flat), th.rearrange(flat), 1.0, gin.rearrange(flat),
                                       ALU.add, ALU.mult).then_inc(gs_done.sem, 1)
                v.wait_ge(*bank_read(f"U{G - 1}", b))
                r = U[:, :, :, DV]

                def per_head(n):
                    return gn[:, n, :].rearrange("p (c h) -> p c h", h=H)

                v.tensor_reduce(per_head(0), U[:, :, :, 0:DV], AX_X, ALU.add).then_inc(gnv.sem, 1)
                v.scalar_tensor_tensor(per_head(1), r, -1.0, r, ALU.mult, ALU.max).then_inc(gnv.sem, 1)
                v.wait_ge(*gnv.count(b, 1))
                v.tensor_scalar(gn[:, 0, :], gn[:, 0, :], 1.0 / DV, None, ALU.mult).then_inc(gnv.sem, 1)
                v.wait_ge(*gnv.count(b, 2))
                v.tensor_tensor(gn[:, 1, :], gn[:, 1, :], nrm[:], ALU.max).then_inc(gnv.sem, 1)
                v.wait_ge(*gnv.count(b, 4))
                v.scalar_tensor_tensor(gn[:, 2, :], gn[:, 1, :], GN_EPS, gn[:, 1, :], ALU.mult,
                                       ALU.mult).then_inc(gnv.sem, 1)
                v.wait_ge(*gnp.count(b, 2))
                v.tensor_reduce(gn[:, 3, :], sq.rearrange("p c (h v) -> p (c h) v", v=DV), AX_X,
                                ALU.add).then_inc(gnv.sem, 1)
                v.wait_ge(*gnv.count(b, 6))
                v.scalar_tensor_tensor(gn[:, 4, :], gn[:, 3, :], 1.0 / DV, gn[:, 2, :], ALU.mult,
                                       ALU.add).then_inc(gnv.sem, 1)
                v.wait_ge(*gs_done.count(b, 1))
                hv = "p c (h v) -> p (c h) v"
                v.wait_ge(*gnp.count(b, 3))
                v.tensor_tensor(sq.rearrange(hv, v=DV), th.rearrange(hv, v=DV),
                                gn[:, 5, :].unsqueeze(2).to_broadcast([P, NT * H, DV]), ALU.mult).then_inc(gnv.sem, 1)
                v.wait_ge(*gnv.count(b, 8))
                v.tensor_tensor(sq, sq, gin, ALU.mult).then_inc(gnv.sem, 1)
                v.wait_ge(*bank_full("sp", b))
                v.wait_ge(*s_spilled.before(b))
                v.tensor_tensor(s_out[:], bankof("sp").rearrange("p (i d) -> p i d", i=NT),
                                b_o[:].unsqueeze(1).to_broadcast([P, NT, D]), ALU.add).then_inc(*read("sp"))

            def row_max(b, h, half):
                for i in (2 * half, 2 * half + 1):
                    use = f"mx{h}_{i}"
                    v.wait_ge(*bank_full(use, b))
                    v.tensor_reduce(mx[:, i, h:h + 1], bankof(use), AX_X, ALU.max).then_inc(*read(use))

            def maxima(b):
                v.wait_ge(*bank_read(f"mx{H - 1}_{NT - 2}", b))
                v.wait_ge(*bank_read(f"mx{H - 1}_{NT - 1}", b))
                v.tensor_scalar(m_hi[:], mx[:], -1.0, None, ALU.mult).then_inc(m_done.sem, 1)
                v.wait_ge(*m_done.count(b, 1))
                v.tensor_copy(m2[:, :, 0, :], m_hi[:].bitcast(F32)).then_inc(m_done.sem, 1)
                v.scalar_tensor_tensor(m2[:, :, 1, :], mx[:], -1.0, m_hi[:].bitcast(F32), ALU.mult,
                                       ALU.subtract).then_inc(m_done.sem, 1)

            def context(b, g):
                use = f"OT{g}"
                v.wait_ge(*bank_full(use, b))
                o = bankof(use).rearrange("p (i m w) -> p i m w", i=NT, w=SLOT)
                if g:
                    v.wait_ge(*bank_read(f"OT{g - 1}", b))
                v.reciprocal(rec[:], o[:, :, :, DK]).then_inc(rec_done.sem, 1)
                v.wait_ge(*rec_done.count(b, g + 1))
                v.tensor_tensor(ctxt[:, :, g * HG * DK:(g + 1) * HG * DK].rearrange("p i (m d) -> p i m d", d=DK),
                                o[:, :, :, 0:DK], rec[:].unsqueeze(3).to_broadcast([P, NT, HG, DK]),
                                ALU.mult).then_inc(*read(use))

            def residual(b):
                v.wait_ge(*bank_full("xp", b))
                v.wait_ge(*xn_b_ld.count(b, 16))
                v.tensor_tensor(X1[:], xn_b[:], bankof("xp").rearrange("p (i d) -> p i d", i=NT),
                                ALU.add).then_inc(*read("xp"))
                v.wait_ge(*rs2_done.count(b, 3))
                v.wait_ge(*bank_read("xp", b))
                for i in range(NT):
                    v.tensor_scalar(h2[:, i, :], X1[:, i, :], rs2[:, 2, i:i + 1], None, ALU.mult).then_inc(h2_done.sem, 1)
                v.wait_ge(*h2hi_done.count(b, 1))
                v.scalar_tensor_tensor(h2_lo[:], bankof("h2T"), colb[:, 5:6], h2_hi[:].bitcast(F32), ALU.mult,
                                       ALU.subtract).then_inc(*read("h2T"))

            def router(b):
                def bc(a):
                    return a.unsqueeze(2).to_broadcast([P, NT, E])

                v.wait_ge(*bank_full("lg", b))
                lgp = bankof("lg")[:, 0:NT * E].rearrange("p (i e) -> p i e", e=E)
                v.tensor_reduce(rt[:, 0, :], lgp, AX_X, ALU.max).then_inc(lgv.sem, 1)
                v.wait_ge(*lgv.count(b, 1))
                v.tensor_tensor(lg[:, 0, :, :], lgp, bc(rt[:, 0, :]), ALU.subtract).then_inc(*read("lg"))
                v.wait_ge(*lga.count(b, 1))
                v.tensor_reduce(rt[:, 1, :], lg[:, 1, :, :], AX_X, ALU.add).then_inc(lgv.sem, 1)
                v.wait_ge(*lgv.count(b, 2))
                v.reciprocal(rt[:, 2, :], rt[:, 1, :]).then_inc(lgv.sem, 1)
                v.wait_ge(*lgv.count(b, 3))
                v.tensor_tensor(lg[:, 1, :, :], lg[:, 1, :, :], bc(rt[:, 2, :]), ALU.mult)
                v.drain()
                for i in range(NT):
                    ins_ = v.max(top[:, i, :], lg[:, 1, i, :])
                v.drain()
                for i in range(NT):
                    ins_ = v.max_index(topi[:, i, :], top[:, i, :], lg[:, 1, i, :])
                ins_.then_inc(lgv.sem, 1)
                v.wait_ge(*lgv.count(b, 4))
                v.tensor_copy(topf[:], topi[:]).then_inc(lgv.sem, 1)
                v.wait_ge(*lgv.count(b, 5))
                v.tensor_tensor(rt[:, 3, :], top[:, :, 1], top[:, :, 0], ALU.subtract).then_inc(lgv.sem, 1)
                v.wait_ge(*lgv.count(b, 6))
                v.wait_ge(*lga.count(b, 2))
                v.tensor_scalar(rt[:, 5, :], rt[:, 4, :], 1.0, None, ALU.add).then_inc(lgv.sem, 1)
                v.wait_ge(*lgv.count(b, 7))
                v.reciprocal(rt[:, 6, :], rt[:, 5, :]).then_inc(lgv.sem, 1)
                v.wait_ge(*lgv.count(b, 8))
                v.tensor_tensor(rt[:, 7, :], rt[:, 4, :], rt[:, 6, :], ALU.mult).then_inc(lgv.sem, 1)
                v.wait_ge(*lgv.count(b, 9))
                v.tensor_tensor(lg[:, 2, :, :], iota[:], bc(topf[:, :, 0]), ALU.is_equal).then_inc(lgv.sem, 1)
                v.wait_ge(*lgv.count(b, 10))
                v.tensor_tensor(lg[:, 3, :, :], iota[:], bc(topf[:, :, 1]), ALU.is_equal).then_inc(lgv.sem, 1)
                v.wait_ge(*lgv.count(b, 11))
                v.tensor_tensor(lg[:, 2, :, :], lg[:, 2, :, :], bc(rt[:, 6, :]), ALU.mult).then_inc(lgw.sem, 1)
                v.tensor_tensor(lg[:, 3, :, :], lg[:, 3, :, :], bc(rt[:, 7, :]), ALU.mult).then_inc(lgw.sem, 1)
                v.wait_ge(*lgw.count(b, 2))
                v.tensor_tensor(lg[:, 3, :, :], lg[:, 2, :, :], lg[:, 3, :, :], ALU.add).then_inc(lgv.sem, 1)

            def gate(b, u):
                v.wait_ge(*th2.count(b, u + 1))
                t = hid[:, u % 3, :]
                v.scalar_tensor_tensor(t, t, 1.0, bankof(f"ga{u}"), ALU.add, ALU.mult).then_inc(*read(f"ga{u}"))

            def up(b, u):
                v.wait_ge(*bank_full(f"up{u}", b))
                v.wait_ge(*bank_read(f"ga{u}", b))
                t = hid[:, u % 3, :]
                v.tensor_tensor(t, t, bankof(f"up{u}"), ALU.mult).then_inc(*read(f"up{u}"))

            def final(b):
                v.wait_ge(*bank_full("mo", b))
                v.wait_ge(*stored.before(b))
                v.tensor_tensor(Y[:], X1[:], bankof("mo").rearrange("p (i d) -> p i d", i=NT),
                                ALU.add).then_inc(*read("mo"))
                v.wait_ge(*tY_done.count(b, 1))
                v.scalar_tensor_tensor(Y[:].rearrange(flat), tY[:].rearrange(flat), 1.0, Y[:].rearrange(flat), ALU.add,
                                       ALU.mult).then_inc(Yv.sem, 1)
                v.wait_ge(*Yv.count(b, 1))
                v.wait_ge(*s_res_ld.count(b, 16))
                v.scalar_tensor_tensor(Y[:].rearrange(flat), Y[:].rearrange(flat), 0.5, s_res[:].rearrange(flat), ALU.mult,
                                       ALU.mult).then_inc(Yv.sem, 1)
                v.wait_ge(*x_res_ld.count(b, 16))
                v.wait_ge(*Yv.count(b, 2))
                v.tensor_tensor(Y[:], Y[:], x_res[:], ALU.add).then_inc(Yv.sem, 1)

            def iteration(i, A, Bs, C, last=False):
                b, c = i - 1, i - 2
                if C:
                    for u in range(U0):
                        gate(c, u)
                        up(c, u)
                if A:
                    norms(i)
                    projections(i)
                    states(i)
                    retention(i)
                    group_norm(i)
                if A and Bs:
                    v.wait_ge(*spilled_r.count(i, 32))
                for n in range(H):
                    g, j = divmod(n, NT)
                    if A:
                        row_max(i, n, 0)
                    if C:
                        gate(c, n + U0)
                    if A:
                        row_max(i, n, 1)
                    if C:
                        up(c, n + U0)
                    if Bs and j == 1 and g:
                        context(b, g - 1)
                if Bs:
                    context(b, G - 1)
                if A:
                    maxima(i)
                if C:
                    final(c)
                if Bs:
                    residual(b)
                    router(b)

            iterations(v, iteration)

        @block.scalar
        def _(a):
            a.wait_ge(loaded.sem, 16 * n_loads[0])

            def front(b):
                a.wait_ge(*bank_full("xnT", b))
                a.copy(xnT[:], bankof("xnT")).then_inc(*read("xnT"))
                a.wait_ge(*bank_full("hT", b))
                a.activation(hT[:], bankof("hT"), ACT.Identity, scale=colb[:, 4:5]).then_inc(*read("hT"))
                a.wait_ge(*spilled_a.before(b))
                a.wait_ge(*bank_full("aq", b))
                a.mul(aq_hi[:], bankof("aq"), float(DK) ** -0.5).then_inc(ahi_done.sem, 1)
                a.wait_ge(*bank_full("ak", b))
                a.copy(ak_hi[:], bankof("ak")).then_inc(ahi_done.sem, 1)
                for c in range(NT - 2, NT):
                    a.wait_ge(*bank_read(f"vg{c}", b))
                a.activation(th, gin, ACT.Tanh, scale=0.5).then_inc(th_done.sem, 1)

            def retention(b):
                for g in range(G):
                    use = f"U{g}"
                    a.wait_ge(*bank_full(use, b))
                    a.copy(U[:, :, g * HG:(g + 1) * HG, :],
                           bankof(use)[:, 0:NT * HG * DV1].rearrange("p (c m v) -> p c m v", c=NT, v=DV1)).then_inc(*read(use))
                for k in range(2):
                    use = f"yT{k}"
                    a.wait_ge(*bank_full(use, b))
                    a.copy(yT[:, k, :], bankof(use)).then_inc(*read(use))

            def attention_v(b):
                a.wait_ge(*bank_full("av", b))
                a.copy(vt[:, :, :, 0:DK], bankof("av").rearrange("p (i h d) -> p i h d", i=NT, h=H)).then_inc(*read("av"))

            def maxima(b):
                a.wait_ge(*bank_full("mT", b))
                a.wait_ge(*m_spilled.before(b))
                a.copy(mTs, bankof("mT")[0:2 * H, :]).then_inc(*read("mT"))

            def exps(b, n, half):
                g, j = divmod(n, NT)
                if n >= 2 and half == 0:
                    g2, j2 = divmod(n - 2, NT)
                    if j2 == NT - 1:
                        a.wait_ge(*bank_full(f"O{g2}", b))
                    else:
                        a.wait_ge(*pv_done.count(b, g2 * (NT - 1) + j2 + 1))
                for m in (2 * half, 2 * half + 1):
                    use = f"sc{g}{j}{m}"
                    a.wait_ge(*bank_full(use, b))
                    a.activation(PT[:, (j % 2) * HG + m, :], bankof(use), ACT.Exp).then_inc(*read(use))

            def attention_sums(b, g):
                a.wait_ge(*bank_full(f"O{g}", b))
                if g:
                    a.wait_ge(*bank_full(f"OT{g - 1}", b))
                a.copy(Os[:], bankof(f"O{g}")).then_inc(*read(f"O{g}"))

            def residual(b):
                a.wait_ge(*bank_full("ctxT", b))
                a.copy(ctxT[:], bankof("ctxT")).then_inc(*read("ctxT"))

            def norm2(b):
                a.wait_ge(*bank_read("xp", b))
                for i in range(NT):
                    a.activation(h2[:, i, :], X1[:, i, :], ACT.Square,
                                 accum_out=rs2[:, 0, i:i + 1]).then_inc(sq2_done.sem, 1)
                a.wait_ge(*bank_full("h2T", b))
                a.activation(h2_hi[:], bankof("h2T"), ACT.Identity, scale=colb[:, 5:6]).then_inc(h2hi_done.sem, 1)

            def router(b):
                a.wait_ge(*bank_read("lg", b))
                a.activation(lg[:, 1, :, :], lg[:, 0, :, :], ACT.Exp).then_inc(lga.sem, 1)
                a.wait_ge(*lgv.count(b, 6))
                a.activation(rt[:, 4, :], rt[:, 3, :], ACT.Exp).then_inc(lga.sem, 1)
                a.wait_ge(*bank_full("wT", b))
                a.wait_ge(*w_spilled.before(b))
                a.copy(wTs, bankof("wT")[0:E, :]).then_inc(*read("wT"))

            def broadcast(b, e):
                if e >= WB:
                    a.wait_ge(*hidw.count(b, NF * (e - WB + 1)))
                a.dma_start(wbc[:, e % WB, :], bass.AP(d_w.tensor, e * S, [[0, P], [1, S]])).then_inc(w_bcast[e % WB].sem, 16)

            def tanh(b, u):
                a.wait_ge(*bank_full(f"ga{u}", b))
                if u >= 3:
                    a.wait_ge(*down_done.count(b, u - 2))
                a.activation(hid[:, u % 3, :], bankof(f"ga{u}"), ACT.Tanh, scale=0.5).then_inc(th2.sem, 1)

            def iteration(i, A, Bs, C, last=False):
                b, c = i - 1, i - 2
                if C:
                    a.wait_ge(*w_spilled.count(c, 16))
                    a.wait_ge(*hidw.before(c))
                    for e in range(WB):
                        broadcast(c, e)
                    for u in range(U0):
                        tanh(c, u)
                if A:
                    front(i)
                    retention(i)
                if A and Bs:
                    a.wait_ge(*gnv.count(i, gnv.per))
                    a.wait_ge(*spilled_r.count(i, 32))
                    a.wait_ge(*qd_done.count(i, 1))
                for n in range(H):
                    if Bs:
                        exps(b, n, 0)
                    if C:
                        u = n + U0
                        tanh(c, u)
                        e = u // NF - 1
                        if u % NF == 1 and e >= 1 and e - 1 + WB < E:
                            broadcast(c, e - 1 + WB)
                    if Bs:
                        exps(b, n, 1)
                        if n % NT == 0 and n:
                            attention_sums(b, n // NT - 1)
                if Bs:
                    attention_sums(b, G - 1)
                if C:
                    a.wait_ge(*bank_full("moe", c))
                    a.copy(moT, bankof("moe")).then_inc(*read("moe"))
                if A:
                    attention_v(i)
                    maxima(i)
                if Bs:
                    residual(b)
                if C:
                    a.wait_ge(*bank_read("mo", c))
                    a.activation(tY[:], Y[:], ACT.Tanh, scale=0.5).then_inc(tY_done.sem, 1)
                if Bs:
                    norm2(b)
                    router(b)

            iterations(a, iteration)

        @block.gpsimd
        def _(p):
            p.wait_ge(inited.sem, 12)
            p.wait_ge(loaded.sem, 16 * n_loads[0])
            half4 = neghalf[:, 0:NT]

            def norms(b):
                p.wait_ge(*mv_done.count(b, NT))
                p.wait_ge(*xn_done.before(b))
                p.wait_ge(*hn_done.before(b))
                var = mv[:, :, 1]
                p.tensor_tensor(lnc[:, 0, :], var, consts[:, 0, :], ALU.add).then_inc(lnf.sem, 1)
                p.wait_ge(*lnf.count(b, 1))
                p.tensor_tensor(lnc[:, 1, :], lnc[:, 0, :], half4, ALU.pow).then_inc(lnf.sem, 1)
                p.wait_ge(*lnf.count(b, 2))
                p.tensor_tensor(lnc[:, 2, :], lnc[:, 1, :], var, ALU.mult).then_inc(lnf.sem, 1)
                p.wait_ge(*lnf.count(b, 3))
                p.tensor_tensor(lnc[:, 3, :], lnc[:, 2, :], lnc[:, 1, :], ALU.mult).then_inc(lnf.sem, 1)
                p.wait_ge(*lnf.count(b, 4))
                p.tensor_tensor(lnc[:, 3, :], lnc[:, 3, :], consts[:, 1, :], ALU.add).then_inc(lnf.sem, 1)
                p.wait_ge(*lnf.count(b, 5))
                p.tensor_tensor(lnc[:, 4, :], lnc[:, 3, :], half4, ALU.pow).then_inc(lnf.sem, 1)
                p.wait_ge(*lnf.count(b, 6))
                p.tensor_tensor(lnc[:, 5, :], lnc[:, 4, :], lnc[:, 1, :], ALU.mult).then_inc(lnf.sem, 1)
                p.wait_ge(*lnf.count(b, 7))

            def rotary(b):
                p.wait_ge(*spilled_r.before(b))
                p.wait_ge(*bank_read("rq", b))
                p.wait_ge(*bank_read("rqs", b))
                p.tensor_tensor(qr[:], rot[:, 0, :], rot[:, 1, :], ALU.add).then_inc(qk_done.sem, 1)
                p.wait_ge(*bank_read("rk", b))
                p.wait_ge(*bank_read("rks", b))
                p.tensor_tensor(rot[:, 2, :], rot[:, 2, :], rot[:, 3, :], ALU.add).then_inc(lnf.sem, 1)
                p.wait_ge(*lnf.count(b, 8))
                p.tensor_tensor(kr[:], rot[:, 2, :], consts[:, 3, 0:1].to_broadcast([P, S]), ALU.mult).then_inc(qk_done.sem, 1)
                p.wait_ge(*qk_done.count(b, 1))
                p.tensor_tensor(qd, qr[:].rearrange("p (i s) -> p i s", i=NT),
                                qdec[:].unsqueeze(1).to_broadcast([P, NT, P]), ALU.mult).then_inc(qd_done.sem, 1)

            def group_norm(b):
                hv = "p c (h v) -> p c h v"
                p.wait_ge(*gnv.count(b, 3))
                p.wait_ge(*gs_done.count(b, 1))
                p.tensor_tensor(th.rearrange(hv, v=DV), U[:, :, :, 0:DV],
                                gn[:, 0, :].rearrange("p (c h) -> p c h", h=H).unsqueeze(3).to_broadcast([P, NT, H, DV]),
                                ALU.subtract).then_inc(gnp.sem, 1)
                p.wait_ge(*gnp.count(b, 1))
                p.tensor_tensor(sq, th, th, ALU.mult).then_inc(gnp.sem, 1)
                p.wait_ge(*gnv.count(b, 7))
                p.tensor_tensor(gn[:, 5, :], gn[:, 4, :], neghalf[:, 0:NT * H], ALU.pow).then_inc(gnp.sem, 1)

            def norm2(b):
                p.wait_ge(*sq2_done.count(b, NT))
                p.tensor_tensor(rs2[:, 1, :], rs2[:, 0, :], consts[:, 2, :], ALU.mult).then_inc(rs2_done.sem, 1)
                p.wait_ge(*rs2_done.count(b, 1))
                p.tensor_tensor(rs2[:, 3, :], rs2[:, 1, :], consts[:, 1, :], ALU.add).then_inc(rs2_done.sem, 1)
                p.wait_ge(*rs2_done.count(b, 2))
                p.tensor_tensor(rs2[:, 2, :], rs2[:, 3, :], half4, ALU.pow).then_inc(rs2_done.sem, 1)

            def weight(b, u):
                p.wait_ge(*bank_read(f"up{u}", b))
                e = u // NF - 1
                p.wait_ge(*w_bcast[e % WB].count(b, 16 * (e // WB + 1)))
                t = hid[:, u % 3, :]
                p.tensor_tensor(t, t, wbc[:, e % WB, :], ALU.mult).then_inc(hidw.sem, 1)

            def iteration(i, A, Bs, C, last=False):
                b, c = i - 1, i - 2
                if A:
                    norms(i)
                    rotary(i)
                    group_norm(i)
                if C:
                    for u in range(NF, UNITS):
                        weight(c, u)
                if Bs:
                    norm2(b)

            iterations(p, iteration)


_OUT = (B, S, D)


def kernel(**inputs):
    import concourse.bacc as _bacc
    from concourse.bass_utils import run_bass_kernel_spmd as _run

    def arr(name):
        return np.ascontiguousarray(inputs[name])

    swap = np.arange(D) ^ 1
    data = {
        "x": arr("L0_attn_x"),
        "Wq": arr("L0_attn_Wq"), "Wq_swapped": np.ascontiguousarray(arr("L0_attn_Wq")[:, swap]),
        "Wk": arr("L0_attn_Wk"), "Wk_swapped": np.ascontiguousarray(arr("L0_attn_Wk")[:, swap]),
        "Wv": arr("L0_attn_Wv"), "Wg": arr("L0_attn_Wg"), "Wo": arr("L0_attn_Wo"),
        "bv": arr("L0_attn_bv"), "bg": arr("L0_attn_bg"), "bo": arr("L0_attn_bo"),
        "columns": np.ascontiguousarray(np.stack(
            [arr("L0_attn_bq"), arr("L0_attn_bq")[swap], arr("L0_attn_bk"), arr("L0_attn_bk")[swap],
             arr("L0_ffn_norm1_w"), arr("L0_ffn_norm2_w")], axis=1)),
    }
    for name in ("wq", "wk", "wv", "wo", "router_w", "sh_gate", "sh_up", "sh_down", "e_gate", "e_up", "e_down"):
        data[name] = arr("L0_ffn_" + name)
    tables = {n: np.ascontiguousarray(t, dtype=np.float32) for n, t in shape_tables().items()}

    nc = _bacc.Bacc("TRN2", target_bir_lowering=False, num_devices=1)
    feed, ins, tabs = {}, {}, {}
    for group, made, prefix in ((data, ins, "in_"), (tables, tabs, "tab_")):
        for name, a in group.items():
            feed[prefix + name] = a
            made[name] = nc.dram_tensor(prefix + name, a.shape, mybir.dt.from_np(a.dtype), kind="ExternalInput").ap()
    out = nc.dram_tensor("out", _OUT, F32, kind="ExternalOutput").ap()
    build(nc, ins, tabs, out)
    r = _run(nc, [feed], core_ids=[0])
    return r.results[0]["out"]
```

```python
from contextlib import ExitStack

import numpy as np

import concourse.bass as bass
from concourse import mybir

ALU = mybir.AluOpType
ACT = mybir.ActivationFunctionType
F32 = mybir.dt.float32
F32R = mybir.dt.float32r
U32 = mybir.dt.uint32
AX_X = mybir.AxisListType.X

P = 128
B, S, D = 16, 512, 128
NT = S // P
H = 16
DK = D // H
DV = 2 * D // H
G = 4
HG = H // G
SLOT = 32
E = 8
FF = 256
NF = FF // P
UNITS = (E + 1) * NF
DV1 = DV + 1
DK1 = DK + 1
ROWS = 3 * DK
MROWS = ROWS + 2
NEXT = 6
U0 = UNITS - H
WB = 2
LN_EPS, RMS_EPS, GN_EPS = 1e-5, 1e-6, 1e-5


def shape_tables():
    f = np.float32
    angle = np.repeat((1.0 / 10000.0 ** np.linspace(0.0, 1.0, DK // 2)).astype(f), 2)
    arg = (np.arange(S, dtype=f)[:, None] * angle[None, :]).astype(f).astype(np.float64)
    sign = np.where(np.arange(DK) % 2 == 0, -1.0, 1.0)
    cos = np.tile(np.cos(arg).T, (H, 1)).astype(f)
    sin = np.tile((np.sin(arg) * sign).T, (H, 1)).astype(f)
    decay = np.log1p(-(2.0 ** (-5.0 - np.arange(H))))
    i = np.arange(P)
    diff = i[None, :] - i[:, None]
    mask = np.where(diff[:, None, :] >= 0, np.exp(decay[None, :, None] * np.maximum(diff, 0)[:, None, :]), 0.0)
    qdec = np.repeat(np.exp(decay[:, None] * (i[None, :] + 1)), DK, axis=0)
    kdec = np.repeat(np.exp(decay[None, :] * (P - 1 - i[:, None])), DK, axis=1) * DK ** -0.5
    cdec = np.repeat(np.exp(decay * P), DK)[:, None]
    slot = (np.arange(D)[:, None] // DK % HG == np.arange(HG)[None, :]) * DK ** -0.5
    bd = (np.arange(D)[:, None] // DK == np.arange(H * DV1)[None, :] // DV1)
    a = np.arange(S)
    sums = -np.expm1(decay[None, :] * (a[:, None] + 1)) / -np.expm1(decay)[None, :]
    nrm = np.sqrt(sums).reshape(NT, P, H).transpose(1, 0, 2).reshape(P, NT * H)
    return {
        "cos": cos, "sin": sin, "mask": mask.reshape(P, H * P), "qdec": qdec, "kdec": kdec, "cdec": cdec,
        "slot": slot, "bd": bd, "nrm": nrm, "ident": np.eye(P), "iota": np.tile(np.arange(E), (P, NT)),
    }


class Signal:

    def __init__(self, sem, per):
        self.sem, self.per = sem, per

    def at(self, b, k):
        return b * self.per + k

    def count(self, b, k):
        return self.sem, self.at(b, k)

    def before(self, b):
        return self.sem, self.at(b, 0)


def bank_uses():
    front = ["xnT", "hT", "rq", "rqs", "rk", "rks", "aq", "ak"] + [f"vg{c}" for c in range(NT)]
    front += ["kT"] + [f"st{c}" for c in range(NT - 1)] + [f"in{c}" for c in range(1, NT)]
    uses = [(n, i % 2) for i, n in enumerate(front)]
    for h in range(H):
        uses += [(f"rs{h}", 0), (f"U{h}", 0)]
        uses += [(f"mx{h}_{i}", 1) for i in range(NT)]
    uses += [("av", 1), ("mT", 0)]
    uses += [("yT0", 2), ("yT1", 3), ("sp", 2)]
    for g in range(G):
        uses += [(f"O{g}", 4)]
        for j in range(NT):
            uses += [(f"sc{g}{j}{m}", 2 + m % 2) for m in range(HG)]
            if j == 1 and g:
                uses += [(f"OT{g - 1}", 2)]
    uses += [(f"OT{G - 1}", 2), ("ctxT", 3), ("xp", 2), ("h2T", 3), ("lg", 2), ("wT", 3)]
    for u in range(UNITS):
        uses += [(f"ga{u}", 5), (f"up{u}", 6)]
    uses += [("moe", 7), ("mo", 5)]
    bank, index, count = {}, {}, [0] * 8
    for name, k in uses:
        bank[name], index[name] = k, count[k]
        count[k] += 1
    return bank, index, count


def build(nc, ins, tabs, out):
    with ExitStack() as ctx:
        def sb(name, shape, dt=F32):
            return ctx.enter_context(nc.sbuf_tensor(name, shape, dt))

        def sig(name, per):
            return Signal(ctx.enter_context(nc.semaphore(name)), per)

        BANK, INDEX, COUNT = bank_uses()
        psum = ctx.enter_context(nc.psum_tensor("psum", [P, 8, 512], F32))
        filled = [sig(f"bank{k}_filled", COUNT[k]) for k in range(8)]
        drained = [sig(f"bank{k}_drained", COUNT[k]) for k in range(8)]

        def bankof(use):
            return psum[:, BANK[use], :]

        ident = sb("ident", [P, P])
        cos, sin = sb("cos", [P, S]), sb("sin", [P, S])
        mask = sb("mask", [P, H, P])
        qdec, kdec, cdec = sb("qdec", [P, P]), sb("kdec", [P, D]), sb("cdec", [P, 1])
        slot = sb("slot", [P, HG])
        bd = sb("bd", [P, H * DV1])
        nrm = sb("nrm", [P, NT * H])
        iota = sb("iota", [P, NT, E])
        w_rq, w_rqs, w_rk, w_rks = (sb(n, [P, D]) for n in ("w_rq", "w_rqs", "w_rk", "w_rks"))
        w_vg = sb("w_vg", [P, 4 * D])
        w_ro = sb("w_ro", [P, 2, D])
        w_aq, w_ak, w_av, w_ao = (sb(n, [P, D]) for n in ("w_aq", "w_ak", "w_av", "w_ao"))
        w_rt = sb("w_rt", [P, E])
        w_rt_hi, w_rt_lo = sb("w_rt_hi", [P, E], F32R), sb("w_rt_lo", [P, E], F32R)
        w_gate_hi, w_gate_lo = (sb(n, [P, E + 1, FF], F32R) for n in ("w_gate_hi", "w_gate_lo"))
        w_up_hi, w_up_lo = (sb(n, [P, E + 1, FF], F32R) for n in ("w_up_hi", "w_up_lo"))
        w_down = sb("w_down", [P, UNITS, D])
        colb = sb("colb", [P, 6])
        b_vg = sb("b_vg", [P, 4 * D])
        b_o = sb("b_o", [P, D])
        neghalf = sb("neghalf", [P, 64])
        consts = sb("consts", [P, 4, NT])
        x_in = sb("x_in", [P, NT, D])
        stats = sb("stats", [P, NT, 6])
        mv = sb("mv", [P, NT, 2])
        lnc = sb("lnc", [P, 6, NT])
        xn, hn = sb("xn", [P, NT, D]), sb("hn", [P, NT, D])
        xnT, hT = sb("xnT", [P, S]), sb("hT", [P, S])
        rot = sb("rot", [P, 4, S])
        kd = rot[:, 0, :].rearrange("p (i d) -> p i d", i=NT)
        qd = rot[:, 3, :].rearrange("p (i s) -> p i s", i=NT)
        qr = sb("qr", [P, S])
        krm = sb("krm", [P, HG, S])
        aq_hi, aq_lo, ak_hi, ak_lo = (sb(n, [P, S], F32R) for n in ("aq_hi", "aq_lo", "ak_hi", "ak_lo"))
        aqp, akp = sb("aqp", [P, G, S], F32R), sb("akp", [P, G, S], F32R)
        state = sb("state", [P, NT - 1, H * DV1])
        vr = sb("vr", [P, NT, H, DV1])
        rsc = sb("rsc", [P, 2, S])
        yT = rsc
        U = sb("U", [P, NT, 2 * D + H])
        Uv, Us = U[:, :, 0:2 * D].rearrange("p c (h v) -> p c h v", h=H), U[:, :, 2 * D:]
        gin = sb("gin", [P, NT, 2 * D])
        arena = sb("arena", [P, 2 * HG * S])
        PT = arena[:].rearrange("p (a n) -> p a n", a=2 * HG)
        th = rot[:, 2:4, :].rearrange("p a n -> p (a n)")
        squares = rot[:, 0, 0:NT * HG * DV].rearrange("p (c m v) -> p c m v", c=NT, m=HG)
        xn_b = arena[:, 4 * S:5 * S].rearrange("p (i d) -> p i d", i=NT)
        gn = sb("gn", [P, 6, NT * H])
        s_out = sb("s_out", [P, NT, D])
        mx = sb("mx", [P, NT, H])
        m_hi = sb("m_hi", [P, NT, H], F32R)
        m2 = sb("m2", [P, NT, 2, H])
        rows_T = sb("rows_T", [2 * SLOT, S])
        mTs = rows_T[0:2 * H, :].bitcast(F32R)
        aqx, akx = sb("aqx", [P, G, S], F32R), sb("akx", [P, G, S], F32R)
        vt = sb("vt", [P, NT, H, DK1])
        Os = sb("Os", [P, S])
        rec = sb("rec", [P, NT, HG])
        ctxt = sb("ctxt", [P, NT, D])
        ctxT = Os
        X1 = sb("X1", [P, NT, D])
        rs2 = sb("rs2", [P, 4, NT])
        h2 = xn_b
        h2_hi, h2_lo = sb("h2_hi", [P, S], F32R), sb("h2_lo", [P, S], F32R)
        lg = sb("lg", [P, 4, NT, E])
        rt = sb("rt", [P, 8, NT])
        top = sb("top", [P, NT, 8])
        topi = sb("topi", [P, NT, 8], U32)
        topf = sb("topf", [P, NT, 8])
        wTs = rows_T[SLOT:SLOT + E, :]
        wbc = sb("wbc", [P, WB, S])
        hid = sb("hid", [P, 3, S])
        x_res, Y = sb("x_res", [P, NT, D]), sb("Y", [P, NT, D])
        RAW = E - 1
        raw_gate = arena[:, 0:(E + 1) * FF].rearrange("p (e f) -> p e f", f=FF)
        raw_up = arena[:, (E + 1) * FF:(E + 1 + RAW) * FF].rearrange("p (e f) -> p e f", f=FF)
        raw_last = Y[:].rearrange("p i d -> p (i d)").rearrange("p (e f) -> p e f", f=FF)
        moT = hid[:, 0, :]
        tY, s_res = (hid[:, k, :].rearrange("p (i d) -> p i d", i=NT) for k in (1, 2))
        d_aq, d_ak = (nc.dram_tensor(n, [H, 3, DK, S], F32, kind="Internal").ap() for n in ("d_aq", "d_ak"))
        d_m = nc.dram_tensor("d_m", [2 * H, S], F32, kind="Internal").ap()
        d_w = nc.dram_tensor("d_w", [E, S], F32, kind="Internal").ap()
        d_xn = nc.dram_tensor("d_xn", [B, P, NT * D], F32, kind="Internal").ap()
        d_s = nc.dram_tensor("d_s", [B, P, NT * D], F32, kind="Internal").ap()

        loaded, late_loaded = sig("first_weights_loaded", 0), sig("later_weights_loaded", 0)
        split_ld = sig("weights_to_split_loaded", 0)
        scaled = sig("weights_scaled", 0)
        split = sig("weights_split", 0)
        inited = sig("constants_written", 0)
        x_ld, x_res_ld, s_res_ld = sig("x_loaded", 16), sig("x_res_loaded", 16), sig("s_res_loaded", 16)
        mv_done = sig("mean_var_done", NT)
        lnf = sig("norm_factors_step", 7)
        xn_done, hn_done = sig("xn_done", NT), sig("hn_done", NT)
        xn_spilled, xn_b_ld = sig("xn_spilled", 16), sig("xn_reloaded", 16)
        s_spilled = sig("retention_out_spilled", 16)
        qk_done = sig("rotary_sums_done", 2)
        krm_done = sig("slot_keys_done", 1)
        ahi_done = sig("attention_qk_high_done", 2)
        spilled_a = sig("attention_qk_spilled", 96)
        slot_a = sig("attention_qk_slotted", 16 * 2 * HG)
        qd_done = sig("decayed_q_done", 1)
        vr_done = sig("retention_v_done", NT)
        th_done, gs_done = sig("gate_tanh_done", 1), sig("gate_silu_done", 1)
        st_done = sig("state_step_done", NT - 2)
        cleared = sig("first_chunk_cleared", 1)
        gnp = sig("group_norm_pool_step", 5 * G)
        gnv = sig("group_norm_vector_step", 7 * G)
        m_done = sig("neg_max_step", 3)
        m_spilled, m_slotted = sig("neg_max_spilled", 16), sig("neg_max_slotted", 16 * HG)
        x_copied = sig("slots_copied", 32)
        pv_done = sig("pv_step_done", G * (NT - 1))
        rec_done = sig("softmax_recip_done", G)
        sq2_done = sig("residual_squares_done", NT)
        rs2_done = sig("rms2_factor_step", 3)
        h2_done = sig("h2_done", NT)
        h2hi_done = sig("h2_high_done", 1)
        lgv = sig("router_vector_step", 12)
        lgw = sig("router_weights_step", 2)
        lga = sig("router_exp_step", 2)
        w_spilled = sig("combine_spilled", 16)
        w_bcast = [sig(f"combine_broadcast_to_slot{k}", 16 * E // WB) for k in range(WB)]
        th2 = sig("expert_tanh_done", UNITS)
        hidw = sig("expert_hidden_weighted", UNITS - NF)
        down_done = sig("down_step_done", UNITS - 1)
        Yv, tY_done = sig("final_vector_step", 3), sig("final_tanh_done", 1)
        stored = sig("output_stored", 16)

        def bank_free(use, b):
            k = BANK[use]
            return drained[k].sem, drained[k].at(b, INDEX[use])

        def bank_full(use, b):
            k = BANK[use]
            return filled[k].sem, filled[k].at(b, INDEX[use] + 1)

        def bank_read(use, b):
            k = BANK[use]
            return drained[k].sem, drained[k].at(b, INDEX[use] + 1)

        def full(use):
            return filled[BANK[use]].sem, 1

        def read(use):
            return drained[BANK[use]].sem, 1

        def iterations(eng, iteration):
            iteration(0, True, False, False)
            iteration(1, True, True, False)
            with eng.Fori(2, B - 1) as i:
                iteration(i, True, True, True)
            iteration(B - 1, True, True, True, last=True)
            iteration(B, False, True, True)
            iteration(B + 1, False, False, True)

        n_loads = {loaded: 0, late_loaded: 0, split_ld: 0}
        flat = "p i n -> p (i n)"
        block = ctx.enter_context(nc.Block())

        @block.sync
        def _(sp):
            def ld(dst, src, signal=loaded):
                sp.dma_start(dst, src).then_inc(signal.sem, 16)
                n_loads[signal] += 1

            def x_tiles(b):
                return ins["x"][bass.ds(b, 1)].rearrange("o (i p) d -> p (o i) d", p=P)

            sp.dma_start(x_in[:], x_tiles(0)).then_inc(x_ld.sem, 16)
            ld(ident[:], tabs["ident"])
            for dst, name in ((w_rq, "Wq"), (w_rqs, "Wq_swapped"), (w_rk, "Wk"), (w_rks, "Wk_swapped"), (w_aq, "wq"),
                              (w_ak, "wk"), (colb, "columns")):
                ld(dst[:], ins[name])
            for dst, name in ((cos, "cos"), (sin, "sin"), (qdec, "qdec")):
                ld(dst[:], tabs[name])
            ld(w_vg[:, 0:2 * D], ins["Wv"])
            ld(w_vg[:, 2 * D:4 * D], ins["Wg"])
            ld(b_vg[:, 0:2 * D], bass.AP(ins["bv"].tensor, 0, [[0, P], [1, 2 * D]]))
            ld(b_vg[:, 2 * D:4 * D], bass.AP(ins["bg"].tensor, 0, [[0, P], [1, 2 * D]]))
            for dst, name in ((slot, "slot"), (kdec, "kdec"), (cdec, "cdec"), (bd, "bd"), (nrm, "nrm")):
                ld(dst[:], tabs[name], late_loaded)
            ld(mask[:], tabs["mask"].rearrange("p (h s) -> p h s", h=H), late_loaded)
            for dst, name in ((w_av, "wv"), (w_ao, "wo"), (w_rt, "router_w")):
                ld(dst[:], ins[name], late_loaded)
            ld(b_o[:], bass.AP(ins["bo"].tensor, 0, [[0, P], [1, D]]), late_loaded)
            ld(w_ro[:], ins["Wo"].rearrange("(a p) n -> p a n", p=P), late_loaded)
            ld(iota[:], tabs["iota"].rearrange("p (i e) -> p i e", e=E), late_loaded)
            ld(w_down[:, 0:NF, :], ins["sh_down"].rearrange("(a p) n -> p a n", p=P), late_loaded)
            ld(w_down[:, NF:, :], ins["e_down"].rearrange("e (a p) n -> p (e a) n", p=P), late_loaded)
            ld(raw_gate[:, 0, :], ins["sh_gate"], split_ld)
            ld(raw_gate[:, 1:, :], ins["e_gate"].rearrange("e p f -> p e f"), split_ld)
            ld(raw_up[:, 0, :], ins["sh_up"], split_ld)
            ld(raw_up[:, 1:, :], ins["e_up"][0:RAW - 1].rearrange("e p f -> p e f"), split_ld)
            ld(raw_last, ins["e_up"][RAW - 1:E].rearrange("e p f -> p e f"), split_ld)

            def slot_qk(b):
                for k, (parts, dst) in enumerate((((aq_hi, aq_hi, aq_lo), d_aq), ((ak_hi, ak_lo, ak_hi), d_ak))):
                    sp.wait_ge(*bank_read(("aq", "ak")[k], b))
                    for n, part in enumerate(parts):
                        sp.dma_start(dst[:, n, :, :], part[:].bitcast(F32)).then_inc(spilled_a.sem, 16)
                sp.wait_ge(*x_copied.before(b))
                sp.wait_ge(*spilled_a.count(b, 96))
                for src, dst in ((d_aq, aqp), (d_ak, akp)):
                    for m in range(HG):
                        sp.dma_start(dst[SLOT * m:SLOT * m + ROWS, :, :].bitcast(F32),
                                     src.rearrange("(g m) k d s -> m (k d) g s", m=HG)[m]).then_inc(slot_a.sem, 16)

            def iteration(i, A, Bs, C, last=False):
                b, c = i - 1, i - 2
                tiles = "o p (i d) -> p (o i) d"
                if A:
                    xn_to = d_xn[bass.ds(i, 1)].rearrange("o p n -> p (o n)")
                    x_next = None if last else x_tiles(i + 1)
                if Bs:
                    s_to = d_s[bass.ds(b, 1)].rearrange("o p n -> p (o n)")
                    xn_from = d_xn[bass.ds(b, 1)].rearrange(tiles, d=D)
                if C:
                    s_from, x_again = d_s[bass.ds(c, 1)].rearrange(tiles, d=D), x_tiles(c)
                    out_to = out[bass.ds(c, 1)].rearrange("o (i p) d -> p (o i) d", p=P)
                if A:
                    sp.wait_ge(*xn_done.count(i, NT))
                    sp.dma_start(xn_to, xn[:].rearrange(flat)).then_inc(xn_spilled.sem, 16)
                    if not last:
                        sp.wait_ge(*hn_done.count(i, NT))
                        sp.dma_start(x_in[:], x_next).then_inc(x_ld.sem, 16)
                if Bs:
                    sp.wait_ge(*bank_read("sp", b))
                    sp.dma_start(s_to, s_out[:].rearrange(flat)).then_inc(s_spilled.sem, 16)
                if C:
                    sp.wait_ge(*Yv.before(c))
                    sp.dma_start(x_res[:], x_again).then_inc(x_res_ld.sem, 16)
                if A:
                    if Bs:
                        sp.wait_ge(*bank_full("sc332", b))
                        sp.wait_ge(*bank_full("sc333", b))
                    sp.wait_ge(*slot_a.count(i, slot_a.per))
                    sp.dma_start(aqx[:].bitcast(F32), aqp[:].bitcast(F32)).then_inc(x_copied.sem, 16)
                    sp.dma_start(akx[:].bitcast(F32), akp[:].bitcast(F32)).then_inc(x_copied.sem, 16)
                if Bs:
                    sp.wait_ge(*bank_full(f"O{G - 1}", b))
                    sp.wait_ge(*xn_spilled.count(b, 16))
                    sp.dma_start(xn_b, xn_from).then_inc(xn_b_ld.sem, 16)
                if C:
                    sp.wait_ge(*s_spilled.count(c, 16))
                    sp.wait_ge(*bank_full("moe", c))
                    sp.dma_start(s_res, s_from).then_inc(s_res_ld.sem, 16)
                if A:
                    sp.wait_ge(*bank_read("mT", i))
                    sp.dma_start(d_m, rows_T[0:2 * H, :]).then_inc(m_spilled.sem, 16)
                    sp.wait_ge(*x_copied.count(i, 32))
                    sp.wait_ge(*m_spilled.count(i, 16))
                    for m in range(HG):
                        sp.dma_start(aqx[SLOT * m + ROWS:SLOT * m + MROWS, :, :].bitcast(F32),
                                     d_m.rearrange("(a g m) s -> m a g s", a=2, m=HG)[m]).then_inc(m_slotted.sem, 16)
                if C:
                    sp.wait_ge(*Yv.count(c, 3))
                    sp.dma_start(out_to, Y[:]).then_inc(stored.sem, 16)
                if A and not last:
                    slot_qk(i + 1)
                if Bs:
                    sp.wait_ge(*bank_read("wT", b))
                    if C:
                        for k in range(WB):
                            sp.wait_ge(*w_bcast[k].count(c, w_bcast[k].per))
                    sp.dma_start(d_w, wTs).then_inc(w_spilled.sem, 16)

            slot_qk(0)
            iterations(sp, iteration)
            sp.wait_ge(stored.sem, 16 * B)

        @block.tensor
        def _(pe):
            pe.wait_ge(loaded.sem, 16 * n_loads[loaded])
            pe.wait_ge(inited.sem, 10)

            def mm(o, l, r, start=True, stop=True, **kw):
                return pe.matmul(o, l, r, start=start, stop=stop, **kw)

            def four(use, b, src, rows=P):
                pe.wait_ge(*bank_free(use, b))
                for i in range(NT):
                    ins_ = pe.transpose(bankof(use)[0:rows, i * P:(i + 1) * P], src(i), ident[:])
                ins_.then_inc(*full(use))

            def transposes(b):
                pe.wait_ge(*xn_done.count(b, NT))
                four("xnT", b, lambda i: xn[:, i, :])
                pe.wait_ge(*hn_done.count(b, NT))
                four("hT", b, lambda i: hn[:, i, :])

            def project(b, use, w, source):
                pe.wait_ge(*bank_read("xnT" if source is xnT else "hT", b))
                pe.wait_ge(*bank_free(use, b))
                mm(bankof(use), w[:], source[:]).then_inc(*full(use))

            def values_gates(b, chunks):
                for c in chunks:
                    use = f"vg{c}"
                    pe.wait_ge(*bank_free(use, b))
                    mm(bankof(use), xnT[:, c * P:(c + 1) * P], w_vg[:]).then_inc(*full(use))

            def keys_transposed(b):
                pe.wait_ge(*qk_done.count(b, 2))
                four("kT", b, lambda i: rot[:, 2, i * P:(i + 1) * P])

            def states(b):
                pe.wait_ge(*bank_read("kT", b))
                for c in range(NT - 1):
                    use = f"st{c}"
                    pe.wait_ge(*bank_free(use, b))
                    pe.wait_ge(*vr_done.count(b, c + 1))
                    mm(bankof(use)[:, 0:H * DV1], kd[:, c, :],
                       vr[:, c, :, :].rearrange("p h v -> p (h v)")).then_inc(*full(use))

            def earlier_chunks(b):
                pe.wait_ge(*bank_read(f"st{NT - 2}", b))
                pe.wait_ge(*st_done.count(b, st_done.per))
                for c in range(1, NT):
                    use = f"in{c}"
                    pe.wait_ge(*bank_free(use, b))
                    if c == 1:
                        pe.wait_ge(*qd_done.count(b, 1))
                    mm(bankof(use)[:, 0:H * DV1], qd[:, c, :], state[:, c - 1, :]).then_inc(*full(use))
                pe.wait_ge(*vr_done.count(b, NT))
                pe.wait_ge(*krm_done.count(b, 1))

            def ret_scores(b, h):
                use = f"rs{h}"
                g, m = divmod(h, HG)
                pe.wait_ge(*bank_free(use, b))
                r = slice(SLOT * g, SLOT * g + SLOT)
                for c in range(NT):
                    ins_ = mm(bankof(use)[:, c * P:(c + 1) * P], krm[r, m, c * P:(c + 1) * P],
                              qr[r, c * P:(c + 1) * P])
                ins_.then_inc(*full(use))

            def ret_sums(b, h):
                use, w = f"U{h}", DV1
                pe.wait_ge(*bank_read(f"rs{h}", b))
                for c in range(NT):
                    ins_ = mm(bankof(use)[:, c * w:(c + 1) * w], rsc[:, h % 2, c * P:(c + 1) * P], vr[:, c, h, :])
                ins_.then_inc(*full(use))

            def gated_transposed(b):
                pe.wait_ge(*gnp.count(b, gnp.per))
                for a in range(2):
                    four(f"yT{a}", b, lambda i: U[:, i, a * D:(a + 1) * D])

            def retention_out(b):
                pe.wait_ge(*bank_free("sp", b))
                pe.wait_ge(*bank_read("yT0", b))
                pe.wait_ge(*bank_read("yT1", b))
                for i in range(NT):
                    for a in range(2):
                        ins_ = mm(bankof("sp")[:, i * D:(i + 1) * D], yT[:, a, i * P:(i + 1) * P], w_ro[:, a, :],
                                  start=(a == 0), stop=(a == 1))
                ins_.then_inc(*full("sp"))

            def max_scores(b, h, i):
                g, m = divmod(h, HG)
                r = slice(SLOT * m, SLOT * m + ROWS)
                use = f"mx{h}_{i}"
                pe.wait_ge(*bank_free(use, b))
                mm(bankof(use), aqp[r, g, i * P:(i + 1) * P], akp[r, g, :]).then_inc(*full(use))

            def attention_v(b):
                pe.wait_ge(*bank_free("av", b))
                for i in range(NT):
                    ins_ = mm(bankof("av")[:, i * D:(i + 1) * D], hT[:, i * P:(i + 1) * P], w_av[:])
                ins_.then_inc(*full("av"))

            def maxima(b):
                pe.wait_ge(*m_done.count(b, 3))
                four("mT", b, lambda i: m2[:, i, :, :].rearrange("p a h -> p (a h)"), rows=2 * H)

            def att_scores(b, g, j, half):
                for m in (2 * half, 2 * half + 1):
                    use = f"sc{g}{j}{m}"
                    r = slice(SLOT * m, SLOT * m + MROWS)
                    pe.wait_ge(*bank_free(use, b))
                    mm(bankof(use), akx[r, g, j * P:(j + 1) * P], aqx[r, g, :]).then_inc(*full(use))

            def att_pv(b, g, j):
                if j == 0:
                    pe.wait_ge(*bank_free(f"O{g}", b))
                pe.wait_ge(*bank_read(f"sc{g}{j}2", b))
                pe.wait_ge(*bank_read(f"sc{g}{j}3", b))
                for m in range(HG):
                    ins_ = mm(bankof(f"O{g}")[SLOT * m:SLOT * m + DK1, :], vt[:, j, g * HG + m, :],
                              PT[:, (j % 2) * HG + m, :], start=(j == 0), stop=(j == NT - 1))
                if j == NT - 1:
                    ins_.then_inc(*full(f"O{g}"))
                else:
                    ins_.then_inc(pv_done.sem, 1)

            def att_out(b, g):
                pe.wait_ge(*bank_read(f"O{g}", b))
                four(f"OT{g}", b, lambda i: Os[:, i * P:(i + 1) * P])

            def residual(b):
                pe.wait_ge(*bank_read("ctxT", b))
                pe.wait_ge(*bank_free("xp", b))
                for i in range(NT):
                    ins_ = mm(bankof("xp")[:, i * D:(i + 1) * D], ctxT[:, i * P:(i + 1) * P], w_ao[:])
                ins_.then_inc(*full("xp"))

            def h2_transposed(b):
                pe.wait_ge(*h2_done.count(b, NT))
                four("h2T", b, lambda i: h2[:, i, :])

            def router(b):
                pe.wait_ge(*bank_read("h2T", b))
                pe.wait_ge(*bank_free("lg", b))
                for i in range(NT):
                    t = slice(i * P, (i + 1) * P)
                    o = bankof("lg")[:, i * E:(i + 1) * E]
                    mm(o, h2_hi[:, t], w_rt_hi[:], stop=False)
                    mm(o, h2_hi[:, t], w_rt_lo[:], start=False, stop=False)
                    ins_ = mm(o, h2_lo[:, t], w_rt_hi[:], start=False)
                ins_.then_inc(*full("lg"))

            def combine(b):
                pe.wait_ge(*lgv.count(b, lgv.per))
                four("wT", b, lambda i: lg[:, 3, i, :], rows=E)

            def hidden(b, u, use, hi, lo):
                e, f = divmod(u, NF)
                w = slice(f * P, (f + 1) * P)
                if u == 0:
                    pe.wait_ge(*bank_read("h2T", b))
                pe.wait_ge(*bank_free(use, b))
                mm(bankof(use), hi[:, e, w], h2_hi[:], stop=False)
                mm(bankof(use), hi[:, e, w], h2_lo[:], start=False, stop=False)
                mm(bankof(use), lo[:, e, w], h2_hi[:], start=False).then_inc(*full(use))

            def gate(b, u):
                hidden(b, u, f"ga{u}", w_gate_hi, w_gate_lo)

            def up(b, u):
                hidden(b, u, f"up{u}", w_up_hi, w_up_lo)

            def down(b, u):
                if u == 0:
                    pe.wait_ge(*bank_free("moe", b))
                if u < NF:
                    pe.wait_ge(*bank_read(f"up{u}", b))
                else:
                    pe.wait_ge(*hidw.count(b, u - NF + 1))
                ins_ = mm(bankof("moe"), w_down[:, u, :], hid[:, u % 3, :], start=(u == 0), stop=(u == UNITS - 1))
                if u == UNITS - 1:
                    ins_.then_inc(*full("moe"))
                else:
                    ins_.then_inc(down_done.sem, 1)

            def iteration(i, A, Bs, C, last=False):
                b, c = i - 1, i - 2
                if A:
                    keys_transposed(i)
                if Bs:
                    gated_transposed(b)
                if A:
                    states(i)
                if Bs:
                    retention_out(b)
                if A:
                    earlier_chunks(i)
                if Bs:
                    pe.wait_ge(*m_slotted.count(b, m_slotted.per))
                    pe.wait_ge(*bank_read("av", b))
                if A:
                    pe.wait_ge(*slot_a.count(i, slot_a.per))
                for n in range(H):
                    g, j = divmod(n, NT)
                    u = n + U0
                    if Bs and n:
                        att_pv(b, *divmod(n - 1, NT))
                    if Bs:
                        att_scores(b, g, j, 0)
                    if A and n:
                        ret_sums(i, n - 1)
                    if A:
                        max_scores(i, n, 0)
                    if C:
                        gate(c, u)
                    if A:
                        ret_scores(i, n)
                        max_scores(i, n, 1)
                    if C:
                        down(c, u - 2)
                    if Bs:
                        att_scores(b, g, j, 1)
                    if A:
                        max_scores(i, n, 2)
                    if C:
                        up(c, u)
                    if A:
                        max_scores(i, n, 3)
                    if Bs and j == 1 and g:
                        att_out(b, g - 1)
                if Bs:
                    att_pv(b, G - 1, NT - 1)
                if A:
                    ret_sums(i, H - 1)
                if Bs:
                    att_out(b, G - 1)
                if C:
                    for u in range(UNITS - 2, UNITS):
                        down(c, u)
                ahead = A and not last
                if Bs:
                    pe.wait_ge(*bank_read(f"OT{G - 1}", b))
                    four("ctxT", b, lambda i: ctxt[:, i, :])
                if A:
                    attention_v(i)
                if C:
                    pe.wait_ge(*bank_read("moe", c))
                    four("mo", c, lambda i: moT[:, i * P:(i + 1) * P])
                if Bs:
                    residual(b)
                if A:
                    maxima(i)
                if ahead:
                    transposes(i + 1)
                    project(i + 1, "rq", w_rq, xnT)
                if Bs:
                    h2_transposed(b)
                if ahead:
                    project(i + 1, "rqs", w_rqs, xnT)
                    project(i + 1, "rk", w_rk, xnT)
                    project(i + 1, "rks", w_rks, xnT)
                    project(i + 1, "aq", w_aq, hT)
                    project(i + 1, "ak", w_ak, hT)
                if Bs:
                    router(b)
                if ahead:
                    values_gates(i + 1, (0, 1))
                if Bs:
                    gate(b, 0)
                    up(b, 0)
                    combine(b)
                if ahead:
                    values_gates(i + 1, (2, 3))
                if Bs:
                    gate(b, 1)
                    up(b, 1)

            transposes(0)
            for use, w, source in (("rq", w_rq, xnT), ("rqs", w_rqs, xnT), ("rk", w_rk, xnT), ("rks", w_rks, xnT),
                                   ("aq", w_aq, hT), ("ak", w_ak, hT)):
                project(0, use, w, source)
            values_gates(0, range(NT))
            pe.wait_ge(late_loaded.sem, 16 * n_loads[late_loaded])
            pe.wait_ge(scaled.sem, 2)
            pe.wait_ge(split.sem, 6)
            iterations(pe, iteration)

        @block.vector
        def _(v):
            v.memset(neghalf[:], -0.5).then_inc(inited.sem, 1)
            for n, value in enumerate((LN_EPS, RMS_EPS, 1.0 / D, float(DK) ** -0.5)):
                v.memset(consts[:, n, :], value).then_inc(inited.sem, 1)
            v.memset(vr[:, :, :, DV:DV1], 1.0).then_inc(inited.sem, 1)
            v.memset(vt[:, :, :, DK:DK1], 1.0).then_inc(inited.sem, 1)
            v.memset(akp[:].bitcast(F32), 1.0).then_inc(inited.sem, 1)
            v.memset(aqp[:].bitcast(F32), 1.0).then_inc(inited.sem, 1)
            v.memset(bankof("O0"), 0.0).then_inc(inited.sem, 1)
            v.wait_ge(inited.sem, 10)
            v.wait_ge(loaded.sem, 16 * n_loads[loaded])

            def prepare_weights():
                v.wait_ge(late_loaded.sem, 16 * n_loads[late_loaded])
                v.tensor_scalar(w_down[:], w_down[:], 0.5, None, ALU.mult).then_inc(scaled.sem, 1)
                v.tensor_scalar(w_ro[:], w_ro[:], 0.5, None, ALU.mult).then_inc(scaled.sem, 1)
                v.wait_ge(split_ld.sem, 16 * n_loads[split_ld])
                v.tensor_copy(w_rt_hi[:], w_rt[:]).then_inc(split.sem, 1)
                v.tensor_copy(w_gate_hi[:], raw_gate).then_inc(split.sem, 1)
                v.tensor_copy(w_up_hi[:, 0:RAW, :], raw_up)
                v.tensor_copy(w_up_hi[:, RAW:, :], raw_last).then_inc(split.sem, 1)
                v.wait_ge(split.sem, 3)
                v.tensor_tensor(w_rt_lo[:], w_rt[:], w_rt_hi[:].bitcast(F32), ALU.subtract).then_inc(split.sem, 1)
                v.tensor_tensor(w_gate_lo[:], raw_gate, w_gate_hi[:].bitcast(F32), ALU.subtract).then_inc(split.sem, 1)
                v.tensor_tensor(w_up_lo[:, 0:RAW, :], raw_up, w_up_hi[:, 0:RAW, :].bitcast(F32), ALU.subtract)
                v.tensor_tensor(w_up_lo[:, RAW:, :], raw_last, w_up_hi[:, RAW:, :].bitcast(F32),
                                ALU.subtract).then_inc(split.sem, 1)
                v.wait_ge(split.sem, 6)

            def norm_stats(b):
                v.wait_ge(*lnf.before(b))
                v.wait_ge(*x_ld.count(b, 16))
                for i in range(NT):
                    v.bn_stats(stats[:, i, :], x_in[:, i, :])
                v.drain()
                for i in range(NT):
                    v.bn_aggr(mv[:, i, :], stats[:, i, :]).then_inc(mv_done.sem, 1)

            def norms(b, first=False):
                v.wait_ge(*lnf.count(b, 7))
                if not first:
                    v.wait_ge(*bank_full("xnT", b - 1))
                    v.wait_ge(*bank_full("hT", b - 1))
                    v.wait_ge(*xn_spilled.before(b))
                for i in range(NT):
                    v.tensor_scalar(xn[:, i, :], x_in[:, i, :], mv[:, i, 0:1], lnc[:, 1, i:i + 1],
                                    ALU.subtract, ALU.mult).then_inc(xn_done.sem, 1)

            def norms_h(b):
                for i in range(NT):
                    v.tensor_scalar(hn[:, i, :], x_in[:, i, :], mv[:, i, 0:1], lnc[:, 5, i:i + 1],
                                    ALU.subtract, ALU.mult).then_inc(hn_done.sem, 1)

            def rotary_term(b, n):
                use, tab = (("rq", cos), ("rqs", sin), ("rk", cos), ("rks", sin))[n]
                if n == 0:
                    v.wait_ge(*qk_done.before(b))
                v.wait_ge(*bank_full(use, b))
                v.scalar_tensor_tensor(rot[:, n, :], bankof(use), colb[:, n:n + 1], tab[:], ALU.add,
                                       ALU.mult).then_inc(*read(use))

            def low_parts(b):
                v.wait_ge(*spilled_a.before(b))
                for use, scale, hi, lo in (("aq", float(DK) ** -0.5, aq_hi, aq_lo), ("ak", 1.0, ak_hi, ak_lo)):
                    v.wait_ge(*ahi_done.count(b, 1 if use == "aq" else 2))
                    v.scalar_tensor_tensor(lo[:], bankof(use), scale, hi[:].bitcast(F32), ALU.mult,
                                           ALU.subtract).then_inc(*read(use))

            def values_gates(b, chunks):
                for c in chunks:
                    use = f"vg{c}"
                    hv = "p (h v) -> p h v"
                    v.wait_ge(*bank_full(use, b))
                    v.tensor_tensor(vr[:, c, :, 0:DV], bankof(use)[:, 0:2 * D].rearrange(hv, h=H),
                                    b_vg[:, 0:2 * D].rearrange(hv, h=H), ALU.add).then_inc(vr_done.sem, 1)
                    if c == 0:
                        v.wait_ge(*gnp.before(b))
                    v.tensor_tensor(gin[:, c, :], bankof(use)[:, 2 * D:4 * D], b_vg[:, 2 * D:4 * D],
                                    ALU.add).then_inc(*read(use))

            def states(b):
                v.wait_ge(*bank_full("kT", b))
                v.wait_ge(*qk_done.count(b, 1))
                v.tensor_tensor(kd, bankof("kT").rearrange("p (i d) -> p i d", i=NT),
                                kdec[:].unsqueeze(1).to_broadcast([P, NT, D]), ALU.mult).then_inc(*read("kT"))
                for c in range(NT - 1):
                    use = f"st{c}"
                    v.wait_ge(*bank_full(use, b))
                    v.tensor_tensor(state[:, c, :], bankof(use)[:, 0:H * DV1], bd[:], ALU.mult).then_inc(*read(use))
                    if c > 0:
                        v.wait_ge(*bank_read(use, b))
                        if c > 1:
                            v.wait_ge(*st_done.count(b, c - 1))
                        v.scalar_tensor_tensor(state[:, c, :], state[:, c - 1, :], cdec[:, 0:1], state[:, c, :],
                                               ALU.mult, ALU.add).then_inc(st_done.sem, 1)

            def ret_mask(b, h):
                cs = "p (c s) -> p c s"
                use = f"rs{h}"
                v.wait_ge(*bank_full(use, b))
                v.tensor_tensor(rsc[:, h % 2, :].rearrange(cs, c=NT), bankof(use).rearrange(cs, c=NT),
                                mask[:, h, :].unsqueeze(1).to_broadcast([P, NT, P]),
                                ALU.mult).then_inc(*read(use))

            def ret_add(b, h):
                use = f"U{h}"
                if h == 0:
                    v.wait_ge(*cleared.count(b, 1))
                    v.wait_ge(*bank_read(f"in{NT - 2}", b))
                    v.wait_ge(*bank_read(f"in{NT - 1}", b))
                v.wait_ge(*bank_full(use, b))
                part = bankof(use)[:, 0:NT * DV1].rearrange("p (c v) -> p c v", v=DV1)
                v.tensor_tensor(Uv[:, :, h, :], Uv[:, :, h, :], part[:, :, 0:DV], ALU.add)
                v.tensor_tensor(Us[:, :, h], Us[:, :, h], part[:, :, DV], ALU.add).then_inc(*read(use))

            def of_group(n, g):
                return gn[:, n, :].rearrange("p (c h) -> p c h", h=H)[:, :, g * HG:(g + 1) * HG]

            def group_means(b, g):
                n0, heads = 7 * g, slice(g * HG, (g + 1) * HG)
                row_sum = Us[:, :, heads]
                v.wait_ge(*bank_read(f"U{(g + 1) * HG - 1}", b))
                v.tensor_reduce(of_group(0, g), Uv[:, :, heads, :], AX_X, ALU.add).then_inc(gnv.sem, 1)
                v.scalar_tensor_tensor(of_group(1, g), row_sum, -1.0, row_sum, ALU.mult, ALU.max).then_inc(gnv.sem, 1)
                v.wait_ge(*gnv.count(b, n0 + 1))
                v.tensor_scalar(of_group(0, g), of_group(0, g), 1.0 / DV, None, ALU.mult).then_inc(gnv.sem, 1)
                v.wait_ge(*gnv.count(b, n0 + 2))
                v.tensor_tensor(of_group(1, g), of_group(1, g), nrm[:].rearrange("p (c h) -> p c h", h=H)[:, :, heads],
                                ALU.max).then_inc(gnv.sem, 1)
                v.wait_ge(*gnv.count(b, n0 + 4))
                v.scalar_tensor_tensor(of_group(2, g), of_group(1, g), GN_EPS, of_group(1, g), ALU.mult,
                                       ALU.mult).then_inc(gnv.sem, 1)

            def gate_silu(b):
                v.wait_ge(*th_done.count(b, 1))
                v.scalar_tensor_tensor(gin[:].rearrange(flat), th, 1.0, gin[:].rearrange(flat),
                                       ALU.add, ALU.mult).then_inc(gs_done.sem, 1)

            def group_variances(b, g):
                v.wait_ge(*gnp.count(b, 5 * g + 2))
                v.tensor_reduce(of_group(3, g), squares, AX_X, ALU.add).then_inc(gnv.sem, 1)
                v.wait_ge(*gnv.count(b, 7 * g + 6))
                v.scalar_tensor_tensor(of_group(4, g), of_group(3, g), 1.0 / DV, of_group(2, g), ALU.mult,
                                       ALU.add).then_inc(gnv.sem, 1)

            def clear_first_chunk(b, Bs):
                if Bs:
                    v.wait_ge(*bank_full("yT1", b - 1))
                v.memset(U[:, 0, :], 0.0).then_inc(cleared.sem, 1)

            def retention_out(b):
                v.wait_ge(*bank_full("sp", b))
                v.wait_ge(*s_spilled.before(b))
                v.tensor_tensor(s_out[:], bankof("sp").rearrange("p (i d) -> p i d", i=NT),
                                b_o[:].unsqueeze(1).to_broadcast([P, NT, D]), ALU.add).then_inc(*read("sp"))

            def row_max(b, h, i):
                use = f"mx{h}_{i}"
                v.wait_ge(*bank_full(use, b))
                v.tensor_reduce(mx[:, i, h:h + 1], bankof(use), AX_X, ALU.max).then_inc(*read(use))

            def maxima(b):
                v.wait_ge(*bank_read(f"mx{H - 1}_{NT - 1}", b))
                v.tensor_scalar(m_hi[:], mx[:], -1.0, None, ALU.mult).then_inc(m_done.sem, 1)
                v.wait_ge(*m_done.count(b, 1))
                v.tensor_copy(m2[:, :, 0, :], m_hi[:].bitcast(F32)).then_inc(m_done.sem, 1)
                v.scalar_tensor_tensor(m2[:, :, 1, :], mx[:], -1.0, m_hi[:].bitcast(F32), ALU.mult,
                                       ALU.subtract).then_inc(m_done.sem, 1)

            def context(b, g):
                use = f"OT{g}"
                v.wait_ge(*bank_full(use, b))
                o = bankof(use).rearrange("p (i m w) -> p i m w", i=NT, w=SLOT)
                if g:
                    v.wait_ge(*bank_read(f"OT{g - 1}", b))
                v.reciprocal(rec[:], o[:, :, :, DK]).then_inc(rec_done.sem, 1)
                v.wait_ge(*rec_done.count(b, g + 1))
                v.tensor_tensor(ctxt[:, :, g * HG * DK:(g + 1) * HG * DK].rearrange("p i (m d) -> p i m d", d=DK),
                                o[:, :, :, 0:DK], rec[:].unsqueeze(3).to_broadcast([P, NT, HG, DK]),
                                ALU.mult).then_inc(*read(use))

            def residual(b, C):
                if C:
                    v.wait_ge(*bank_read("mo", b - 1))
                v.wait_ge(*bank_full("xp", b))
                v.wait_ge(*xn_b_ld.count(b, 16))
                v.tensor_tensor(X1[:], xn_b, bankof("xp").rearrange("p (i d) -> p i d", i=NT),
                                ALU.add).then_inc(*read("xp"))

            def norm2(b):
                v.wait_ge(*rs2_done.count(b, 3))
                v.wait_ge(*bank_read("xp", b))
                for i in range(NT):
                    v.tensor_scalar(h2[:, i, :], X1[:, i, :], rs2[:, 2, i:i + 1], None, ALU.mult).then_inc(h2_done.sem, 1)

            def split_h2(b):
                v.wait_ge(*h2hi_done.count(b, 1))
                v.scalar_tensor_tensor(h2_lo[:], bankof("h2T"), colb[:, 5:6], h2_hi[:].bitcast(F32), ALU.mult,
                                       ALU.subtract).then_inc(*read("h2T"))

            def router(b):
                def bc(a):
                    return a.unsqueeze(2).to_broadcast([P, NT, E])

                v.wait_ge(*bank_full("lg", b))
                lgp = bankof("lg")[:, 0:NT * E].rearrange("p (i e) -> p i e", e=E)
                v.tensor_reduce(rt[:, 0, :], lgp, AX_X, ALU.max).then_inc(lgv.sem, 1)
                v.wait_ge(*lgv.count(b, 1))
                v.tensor_tensor(lg[:, 0, :, :], lgp, bc(rt[:, 0, :]), ALU.subtract).then_inc(*read("lg"))
                v.wait_ge(*lga.count(b, 1))
                v.tensor_reduce(rt[:, 1, :], lg[:, 1, :, :], AX_X, ALU.add).then_inc(lgv.sem, 1)
                v.wait_ge(*lgv.count(b, 2))
                v.reciprocal(rt[:, 2, :], rt[:, 1, :]).then_inc(lgv.sem, 1)
                v.wait_ge(*lgv.count(b, 3))
                v.tensor_tensor(lg[:, 1, :, :], lg[:, 1, :, :], bc(rt[:, 2, :]), ALU.mult)
                v.drain()
                for i in range(NT):
                    ins_ = v.max(top[:, i, :], lg[:, 1, i, :])
                v.drain()
                for i in range(NT):
                    ins_ = v.max_index(topi[:, i, :], top[:, i, :], lg[:, 1, i, :])
                ins_.then_inc(lgv.sem, 1)
                v.wait_ge(*lgv.count(b, 4))
                v.tensor_copy(topf[:], topi[:]).then_inc(lgv.sem, 1)
                v.wait_ge(*lgv.count(b, 5))
                v.tensor_tensor(rt[:, 3, :], top[:, :, 1], top[:, :, 0], ALU.subtract).then_inc(lgv.sem, 1)
                v.wait_ge(*lgv.count(b, 6))
                v.wait_ge(*lga.count(b, 2))
                v.tensor_scalar(rt[:, 5, :], rt[:, 4, :], 1.0, None, ALU.add).then_inc(lgv.sem, 1)
                v.wait_ge(*lgv.count(b, 7))
                v.reciprocal(rt[:, 6, :], rt[:, 5, :]).then_inc(lgv.sem, 1)
                v.wait_ge(*lgv.count(b, 8))
                v.tensor_tensor(rt[:, 7, :], rt[:, 4, :], rt[:, 6, :], ALU.mult).then_inc(lgv.sem, 1)
                v.wait_ge(*lgv.count(b, 9))
                v.tensor_tensor(lg[:, 2, :, :], iota[:], bc(topf[:, :, 0]), ALU.is_equal).then_inc(lgv.sem, 1)
                v.wait_ge(*lgv.count(b, 10))
                v.tensor_tensor(lg[:, 3, :, :], iota[:], bc(topf[:, :, 1]), ALU.is_equal).then_inc(lgv.sem, 1)
                v.wait_ge(*lgv.count(b, 11))
                v.tensor_tensor(lg[:, 2, :, :], lg[:, 2, :, :], bc(rt[:, 6, :]), ALU.mult).then_inc(lgw.sem, 1)
                v.tensor_tensor(lg[:, 3, :, :], lg[:, 3, :, :], bc(rt[:, 7, :]), ALU.mult).then_inc(lgw.sem, 1)
                v.wait_ge(*lgw.count(b, 2))
                v.tensor_tensor(lg[:, 3, :, :], lg[:, 2, :, :], lg[:, 3, :, :], ALU.add).then_inc(lgv.sem, 1)

            def gate(b, u):
                v.wait_ge(*th2.count(b, u + 1))
                t = hid[:, u % 3, :]
                v.scalar_tensor_tensor(t, t, 1.0, bankof(f"ga{u}"), ALU.add, ALU.mult).then_inc(*read(f"ga{u}"))

            def up(b, u):
                v.wait_ge(*bank_full(f"up{u}", b))
                v.wait_ge(*bank_read(f"ga{u}", b))
                t = hid[:, u % 3, :]
                v.tensor_tensor(t, t, bankof(f"up{u}"), ALU.mult).then_inc(*read(f"up{u}"))

            def final(b):
                v.wait_ge(*bank_full("mo", b))
                v.wait_ge(*stored.before(b))
                v.tensor_tensor(Y[:], X1[:], bankof("mo").rearrange("p (i d) -> p i d", i=NT),
                                ALU.add).then_inc(*read("mo"))

            def gated(b):
                v.wait_ge(*tY_done.count(b, 1))
                v.scalar_tensor_tensor(Y[:].rearrange(flat), tY.rearrange(flat), 1.0, Y[:].rearrange(flat), ALU.add,
                                       ALU.mult).then_inc(Yv.sem, 1)
                v.wait_ge(*Yv.count(b, 1))
                v.wait_ge(*s_res_ld.count(b, 16))
                v.scalar_tensor_tensor(Y[:].rearrange(flat), Y[:].rearrange(flat), 0.5, s_res.rearrange(flat), ALU.mult,
                                       ALU.mult).then_inc(Yv.sem, 1)
                v.wait_ge(*x_res_ld.count(b, 16))
                v.wait_ge(*Yv.count(b, 2))
                v.tensor_tensor(Y[:], Y[:], x_res[:], ALU.add).then_inc(Yv.sem, 1)

            def iteration(i, A, Bs, C, last=False):
                b, c = i - 1, i - 2
                if A:
                    states(i)
                if Bs:
                    retention_out(b)
                if A:
                    clear_first_chunk(i, Bs)
                for n in range(H):
                    g, j = divmod(n, NT)
                    if A and n:
                        ret_add(i, n - 1)
                    if A:
                        row_max(i, n, 0)
                    if C:
                        gate(c, n + U0)
                    if A:
                        row_max(i, n, 1)
                        ret_mask(i, n)
                        row_max(i, n, 2)
                    if C:
                        up(c, n + U0)
                    if A:
                        row_max(i, n, 3)
                    if Bs and j == 1 and g:
                        context(b, g - 1)
                    if A and n == 0:
                        gate_silu(i)
                    if A and j == 0 and g:
                        group_means(i, g - 1)
                    if A and j == 1 and g:
                        group_variances(i, g - 1)
                    if A and not last and n == NEXT:
                        norm_stats(i + 1)
                    if A and not last and n == NEXT + 1:
                        norms(i + 1)
                    if A and not last and n == NEXT + 4:
                        norms_h(i + 1)
                ahead = A and not last
                if A:
                    ret_add(i, H - 1)
                if Bs:
                    context(b, G - 1)
                if A:
                    group_means(i, G - 1)
                    maxima(i)
                if C:
                    final(c)
                if Bs:
                    residual(b, C)
                if A:
                    group_variances(i, G - 1)
                if Bs:
                    norm2(b)
                if C:
                    gated(c)
                if ahead:
                    rotary_term(i + 1, 0)
                    rotary_term(i + 1, 1)
                    rotary_term(i + 1, 2)
                if Bs:
                    split_h2(b)
                if ahead:
                    rotary_term(i + 1, 3)
                    low_parts(i + 1)
                if Bs:
                    router(b)
                if ahead:
                    values_gates(i + 1, (0, 1))
                if Bs:
                    gate(b, 0)
                    up(b, 0)
                if ahead:
                    values_gates(i + 1, (2, 3))
                if Bs:
                    gate(b, 1)
                    up(b, 1)

            norm_stats(0)
            norms(0, first=True)
            norms_h(0)
            for n in range(4):
                rotary_term(0, n)
            low_parts(0)
            values_gates(0, range(NT))
            prepare_weights()
            iterations(v, iteration)

        @block.scalar
        def _(a):
            a.wait_ge(loaded.sem, 16 * n_loads[loaded])

            def transposed(b):
                a.wait_ge(*bank_full("xnT", b))
                a.copy(xnT[:], bankof("xnT")).then_inc(*read("xnT"))
                a.wait_ge(*bank_full("hT", b))
                a.activation(hT[:], bankof("hT"), ACT.Identity, scale=colb[:, 4:5]).then_inc(*read("hT"))

            def high_parts(b):
                a.wait_ge(*spilled_a.before(b))
                a.wait_ge(*bank_full("aq", b))
                a.mul(aq_hi[:], bankof("aq"), float(DK) ** -0.5).then_inc(ahi_done.sem, 1)
                a.wait_ge(*bank_full("ak", b))
                a.copy(ak_hi[:], bankof("ak")).then_inc(ahi_done.sem, 1)

            def slot_keys(b):
                a.wait_ge(*filled[BANK["mT"]].before(b))
                a.wait_ge(*qk_done.count(b, 2))
                for m in range(HG):
                    ins_ = a.activation(krm[:, m, :], rot[:, 2, :], ACT.Identity, scale=slot[:, m:m + 1])
                ins_.then_inc(krm_done.sem, 1)

            def earlier_chunks(b):
                for c in range(1, NT):
                    use = f"in{c}"
                    a.wait_ge(*bank_full(use, b))
                    part = bankof(use)[:, 0:H * DV1].rearrange("p (h v) -> p h v", v=DV1)
                    a.copy(Uv[:, c, :, :], part[:, :, 0:DV])
                    a.copy(Us[:, c, :], part[:, :, DV]).then_inc(*read(use))

            def gate_tanh(b):
                for c in range(NT - 2, NT):
                    a.wait_ge(*bank_read(f"vg{c}", b))
                a.activation(th, gin[:], ACT.Tanh, scale=0.5).then_inc(th_done.sem, 1)

            def yT_copy(b):
                for k in range(2):
                    use = f"yT{k}"
                    a.wait_ge(*bank_full(use, b))
                    a.copy(yT[:, k, :], bankof(use)).then_inc(*read(use))

            def attention_v(b):
                a.wait_ge(*bank_full("av", b))
                a.copy(vt[:, :, :, 0:DK], bankof("av").rearrange("p (i h d) -> p i h d", i=NT, h=H)).then_inc(*read("av"))

            def maxima(b):
                a.wait_ge(*bank_full("mT", b))
                a.wait_ge(*m_spilled.before(b))
                a.copy(mTs, bankof("mT")[0:2 * H, :]).then_inc(*read("mT"))

            def exps(b, n, half):
                g, j = divmod(n, NT)
                if n >= 2 and half == 0:
                    g2, j2 = divmod(n - 2, NT)
                    if j2 == NT - 1:
                        a.wait_ge(*bank_full(f"O{g2}", b))
                    else:
                        a.wait_ge(*pv_done.count(b, g2 * (NT - 1) + j2 + 1))
                for m in (2 * half, 2 * half + 1):
                    use = f"sc{g}{j}{m}"
                    a.wait_ge(*bank_full(use, b))
                    a.activation(PT[:, (j % 2) * HG + m, :], bankof(use), ACT.Exp).then_inc(*read(use))

            def attention_sums(b, g):
                a.wait_ge(*bank_full(f"O{g}", b))
                if g:
                    a.wait_ge(*bank_full(f"OT{g - 1}", b))
                a.copy(Os[:], bankof(f"O{g}")).then_inc(*read(f"O{g}"))

            def residual(b):
                a.wait_ge(*bank_full("ctxT", b))
                a.copy(ctxT[:], bankof("ctxT")).then_inc(*read("ctxT"))

            def norm2(b):
                a.wait_ge(*bank_read("xp", b))
                for i in range(NT):
                    a.activation(h2[:, i, :], X1[:, i, :], ACT.Square,
                                 accum_out=rs2[:, 0, i:i + 1]).then_inc(sq2_done.sem, 1)

            def h2_high(b):
                a.wait_ge(*bank_full("h2T", b))
                a.activation(h2_hi[:], bankof("h2T"), ACT.Identity, scale=colb[:, 5:6]).then_inc(h2hi_done.sem, 1)

            def router(b):
                a.wait_ge(*bank_read("lg", b))
                a.activation(lg[:, 1, :, :], lg[:, 0, :, :], ACT.Exp).then_inc(lga.sem, 1)
                a.wait_ge(*lgv.count(b, 6))
                a.activation(rt[:, 4, :], rt[:, 3, :], ACT.Exp).then_inc(lga.sem, 1)
                a.wait_ge(*bank_full("wT", b))
                a.wait_ge(*w_spilled.before(b))
                a.copy(wTs, bankof("wT")[0:E, :]).then_inc(*read("wT"))

            def broadcast(b, e):
                if e >= WB:
                    a.wait_ge(*hidw.count(b, NF * (e - WB + 1)))
                a.dma_start(wbc[:, e % WB, :], bass.AP(d_w.tensor, e * S, [[0, P], [1, S]])).then_inc(w_bcast[e % WB].sem, 16)

            def next_weights(b, u):
                e = u // NF - 1
                if u % NF == 1 and e >= 1 and e - 1 + WB < E:
                    broadcast(b, e - 1 + WB)

            def tanh(b, u):
                a.wait_ge(*bank_full(f"ga{u}", b))
                if u >= 3:
                    a.wait_ge(*down_done.count(b, u - 2))
                a.activation(hid[:, u % 3, :], bankof(f"ga{u}"), ACT.Tanh, scale=0.5).then_inc(th2.sem, 1)

            def iteration(i, A, Bs, C, last=False):
                b, c = i - 1, i - 2
                if A:
                    slot_keys(i)
                if Bs:
                    yT_copy(b)
                if C:
                    a.wait_ge(*w_spilled.count(c, 16))
                    a.wait_ge(*hidw.before(c))
                    for e in range(WB):
                        broadcast(c, e)
                if A:
                    earlier_chunks(i)
                    gate_tanh(i)
                for n in range(H):
                    u = n + U0
                    if Bs:
                        exps(b, n, 0)
                    if C:
                        next_weights(c, u)
                        tanh(c, u)
                    if Bs:
                        exps(b, n, 1)
                        if n % NT == 0 and n:
                            attention_sums(b, n // NT - 1)
                if Bs:
                    attention_sums(b, G - 1)
                if C:
                    a.wait_ge(*bank_full("moe", c))
                    a.copy(moT, bankof("moe")).then_inc(*read("moe"))
                if Bs:
                    residual(b)
                if A:
                    attention_v(i)
                    maxima(i)
                if Bs:
                    norm2(b)
                ahead = A and not last
                if ahead:
                    transposed(i + 1)
                if C:
                    a.wait_ge(*bank_read("mo", c))
                    a.activation(tY, Y[:], ACT.Tanh, scale=0.5).then_inc(tY_done.sem, 1)
                if Bs:
                    h2_high(b)
                if ahead:
                    high_parts(i + 1)
                if Bs:
                    router(b)
                    a.wait_ge(*Yv.before(b))
                    for u in range(U0):
                        tanh(b, u)

            transposed(0)
            high_parts(0)
            a.wait_ge(late_loaded.sem, 16 * n_loads[late_loaded])
            iterations(a, iteration)

        @block.gpsimd
        def _(p):
            p.wait_ge(inited.sem, 10)
            p.wait_ge(loaded.sem, 16 * n_loads[loaded])
            half4 = neghalf[:, 0:NT]

            def norms(b):
                p.wait_ge(*mv_done.count(b, NT))
                p.wait_ge(*xn_done.before(b))
                p.wait_ge(*hn_done.before(b))
                var = mv[:, :, 1]
                p.tensor_tensor(lnc[:, 0, :], var, consts[:, 0, :], ALU.add).then_inc(lnf.sem, 1)
                p.wait_ge(*lnf.count(b, 1))
                p.tensor_tensor(lnc[:, 1, :], lnc[:, 0, :], half4, ALU.pow).then_inc(lnf.sem, 1)
                p.wait_ge(*lnf.count(b, 2))
                p.tensor_tensor(lnc[:, 2, :], lnc[:, 1, :], var, ALU.mult).then_inc(lnf.sem, 1)
                p.wait_ge(*lnf.count(b, 3))
                p.tensor_tensor(lnc[:, 3, :], lnc[:, 2, :], lnc[:, 1, :], ALU.mult).then_inc(lnf.sem, 1)
                p.wait_ge(*lnf.count(b, 4))
                p.tensor_tensor(lnc[:, 3, :], lnc[:, 3, :], consts[:, 1, :], ALU.add).then_inc(lnf.sem, 1)
                p.wait_ge(*lnf.count(b, 5))
                p.tensor_tensor(lnc[:, 4, :], lnc[:, 3, :], half4, ALU.pow).then_inc(lnf.sem, 1)
                p.wait_ge(*lnf.count(b, 6))
                p.tensor_tensor(lnc[:, 5, :], lnc[:, 4, :], lnc[:, 1, :], ALU.mult).then_inc(lnf.sem, 1)
                p.wait_ge(*lnf.count(b, 7))

            def rotary(b):
                p.wait_ge(*bank_read("rq", b))
                p.wait_ge(*bank_read("rqs", b))
                p.tensor_tensor(qr[:], rot[:, 0, :], rot[:, 1, :], ALU.add).then_inc(qk_done.sem, 1)
                p.wait_ge(*bank_read("rk", b))
                p.wait_ge(*bank_read("rks", b))
                p.tensor_tensor(rot[:, 2, :], rot[:, 2, :], rot[:, 3, :], ALU.add).then_inc(qk_done.sem, 1)
                p.wait_ge(*qk_done.count(b, 2))
                p.tensor_tensor(qd, qr[:].rearrange("p (i s) -> p i s", i=NT),
                                qdec[:].unsqueeze(1).to_broadcast([P, NT, P]), ALU.mult).then_inc(qd_done.sem, 1)

            def centre(b, g):
                heads = slice(g * HG, (g + 1) * HG)
                sums = Uv[:, :, heads, :]
                mean = gn[:, 0, :].rearrange("p (c h) -> p c h", h=H)[:, :, heads]
                p.wait_ge(*gnv.count(b, 7 * g + 3))
                p.tensor_tensor(sums, sums, mean.unsqueeze(3).to_broadcast([P, NT, HG, DV]),
                                ALU.subtract).then_inc(gnp.sem, 1)
                p.wait_ge(*gnp.count(b, 5 * g + 1))
                p.tensor_tensor(squares, sums, sums, ALU.mult).then_inc(gnp.sem, 1)

            def scale(b, g):
                heads = slice(g * HG, (g + 1) * HG)
                sums = Uv[:, :, heads, :]
                var, factor = (gn[:, n, :].rearrange("p (c h) -> p c h", h=H)[:, :, heads] for n in (4, 5))
                p.wait_ge(*gnv.count(b, 7 * (g + 1)))
                p.tensor_tensor(factor, var, neghalf[:, 0:NT * HG].rearrange("p (c m) -> p c m", c=NT),
                                ALU.pow).then_inc(gnp.sem, 1)
                p.wait_ge(*gnp.count(b, 5 * g + 3))
                p.tensor_tensor(sums, sums, factor.unsqueeze(3).to_broadcast([P, NT, HG, DV]),
                                ALU.mult).then_inc(gnp.sem, 1)
                p.wait_ge(*gs_done.count(b, 1))
                p.wait_ge(*gnp.count(b, 5 * g + 4))
                p.tensor_tensor(sums, sums, gin[:, :, g * HG * DV:(g + 1) * HG * DV].rearrange(
                    "p c (m v) -> p c m v", v=DV), ALU.mult).then_inc(gnp.sem, 1)

            def norm2(b):
                p.wait_ge(*sq2_done.count(b, NT))
                p.tensor_tensor(rs2[:, 1, :], rs2[:, 0, :], consts[:, 2, :], ALU.mult).then_inc(rs2_done.sem, 1)
                p.wait_ge(*rs2_done.count(b, 1))
                p.tensor_tensor(rs2[:, 3, :], rs2[:, 1, :], consts[:, 1, :], ALU.add).then_inc(rs2_done.sem, 1)
                p.wait_ge(*rs2_done.count(b, 2))
                p.tensor_tensor(rs2[:, 2, :], rs2[:, 3, :], half4, ALU.pow).then_inc(rs2_done.sem, 1)

            def weight(b, u):
                p.wait_ge(*bank_read(f"up{u}", b))
                e = u // NF - 1
                p.wait_ge(*w_bcast[e % WB].count(b, 16 * (e // WB + 1)))
                t = hid[:, u % 3, :]
                p.tensor_tensor(t, t, wbc[:, e % WB, :], ALU.mult).then_inc(hidw.sem, 1)

            def iteration(i, A, Bs, C, last=False):
                b, c = i - 1, i - 2
                for n in range(H):
                    if C:
                        weight(c, n + U0)
                    if A and n and n % HG == 0:
                        centre(i, n // HG - 1)
                    if A and n > HG and n % HG == 1:
                        scale(i, n // HG - 1)
                    if A and not last and n == NEXT:
                        norms(i + 1)
                if A:
                    centre(i, G - 1)
                if Bs:
                    norm2(b)
                if A:
                    scale(i, G - 1)
                if A and not last:
                    rotary(i + 1)

            norms(0)
            rotary(0)
            iterations(p, iteration)


_OUT = (B, S, D)


def kernel(**inputs):
    import concourse.bacc as _bacc
    from concourse.bass_utils import run_bass_kernel_spmd as _run

    def arr(name):
        return np.ascontiguousarray(inputs[name])

    swap = np.arange(D) ^ 1
    data = {
        "x": arr("L0_attn_x"),
        "Wq": arr("L0_attn_Wq"), "Wq_swapped": np.ascontiguousarray(arr("L0_attn_Wq")[:, swap]),
        "Wk": arr("L0_attn_Wk"), "Wk_swapped": np.ascontiguousarray(arr("L0_attn_Wk")[:, swap]),
        "Wv": arr("L0_attn_Wv"), "Wg": arr("L0_attn_Wg"), "Wo": arr("L0_attn_Wo"),
        "bv": arr("L0_attn_bv"), "bg": arr("L0_attn_bg"), "bo": arr("L0_attn_bo"),
        "columns": np.ascontiguousarray(np.stack(
            [arr("L0_attn_bq"), arr("L0_attn_bq")[swap], arr("L0_attn_bk"), arr("L0_attn_bk")[swap],
             arr("L0_ffn_norm1_w"), arr("L0_ffn_norm2_w")], axis=1)),
    }
    for name in ("wq", "wk", "wv", "wo", "router_w", "sh_gate", "sh_up", "sh_down", "e_gate", "e_up", "e_down"):
        data[name] = arr("L0_ffn_" + name)
    tables = {n: np.ascontiguousarray(t, dtype=np.float32) for n, t in shape_tables().items()}

    nc = _bacc.Bacc("TRN2", target_bir_lowering=False, num_devices=1)
    feed, ins, tabs = {}, {}, {}
    for group, made, prefix in ((data, ins, "in_"), (tables, tabs, "tab_")):
        for name, a in group.items():
            feed[prefix + name] = a
            made[name] = nc.dram_tensor(prefix + name, a.shape, mybir.dt.from_np(a.dtype), kind="ExternalInput").ap()
    out = nc.dram_tensor("out", _OUT, F32, kind="ExternalOutput").ap()
    build(nc, ins, tabs, out)
    r = _run(nc, [feed], core_ids=[0])
    return r.results[0]["out"]
```
